# Optimizing a Trainium2 kernel written in Bass

```python
import numpy as np
import jax
import jax.numpy as jnp

def _softmax(x, axis=-1):
    return jax.nn.softmax(x, axis=axis)

def _gelu(x):
    return jax.nn.gelu(x, approximate=True)

def _silu(x):
    return jax.nn.silu(x)

def _sigmoid(x):
    return jax.nn.sigmoid(x)

def _layernorm(x, axis=-1, eps=1e-05):
    m = jnp.mean(x, axis=axis, keepdims=True)
    v = jnp.var(x, axis=axis, keepdims=True)
    return (x - m) / jnp.sqrt(v + eps)

def _scatter_add(tgt, idx, src, axis=0):
    return tgt.at[idx].add(src)

def _segment_sum(src, seg, n):
    return jax.ops.segment_sum(src, seg, n)
kernel_name = 'mk_sandwich_d1_jaxref_r4_2d07e9'

def setup_inputs(seed: int=0):
    np.random.seed(seed)
    _w = jnp.asarray

    def _L0_attn_setup():
        import jax, jax.numpy as jnp
        import numpy as np
        D_OUT = 256
        key = jax.random.key(seed)
        k1, k2 = jax.random.split(key)
        x = jax.random.normal(k1, (4, 512, 256), dtype=jnp.float32)
        W_qkv = jax.random.normal(k2, (256, 3 * D_OUT), dtype=jnp.float32) * 0.02
        return {'x': x, 'W_qkv': W_qkv}
    _L0_attn_in = _L0_attn_setup()

    def _L0_ffn_setup():
        import jax, jax.numpy as jnp
        import numpy as np
        TOP_K = 2
        NUM_EXPERTS = 8
        key = jax.random.key(seed)
        ks = jax.random.split(key, 8)
        h, d, ds, E = (256, 128, 256, NUM_EXPERTS)
        s = 1.0 / np.sqrt(h)
        return {'x': jax.random.normal(ks[0], (2, 512, h), jnp.float32), 'router': jax.random.normal(ks[1], (h, E), jnp.float32) * s, 'experts_gate': jax.random.normal(ks[2], (E, h, d), jnp.float32) * s, 'experts_up': jax.random.normal(ks[3], (E, h, d), jnp.float32) * s, 'experts_down': jax.random.normal(ks[4], (E, d, h), jnp.float32) * (1.0 / np.sqrt(d)), 'shared_gate': jax.random.normal(ks[5], (h, ds), jnp.float32) * s, 'shared_up': jax.random.normal(ks[6], (h, ds), jnp.float32) * s, 'shared_down': jax.random.normal(ks[7], (ds, h), jnp.float32) * (1.0 / np.sqrt(ds))}
    _L0_ffn_in = _L0_ffn_setup()
    _d = {'L0_attn_x': _L0_attn_in['x'], 'L0_attn_W_qkv': _L0_attn_in['W_qkv'], 'L0_ffn_router': _L0_ffn_in['router'], 'L0_ffn_experts_gate': _L0_ffn_in['experts_gate'], 'L0_ffn_experts_up': _L0_ffn_in['experts_up'], 'L0_ffn_experts_down': _L0_ffn_in['experts_down'], 'L0_ffn_shared_gate': _L0_ffn_in['shared_gate'], 'L0_ffn_shared_up': _L0_ffn_in['shared_up'], 'L0_ffn_shared_down': _L0_ffn_in['shared_down']}
    _x0 = _d['L0_attn_x']
    _d['L0_attn_x'] = jax.random.normal(jax.random.fold_in(jax.random.key(seed), 1), (32, 512, 256), dtype=_x0.dtype)
    del _x0
    return _d

def reference(L0_attn_x, L0_attn_W_qkv, L0_ffn_router, L0_ffn_experts_gate, L0_ffn_experts_up, L0_ffn_experts_down, L0_ffn_shared_gate, L0_ffn_shared_up, L0_ffn_shared_down):

    def _L0_attn_ref(x, W_qkv):
        import jax, jax.numpy as jnp
        import numpy as np
        D_OUT = 256
        B, N, _ = x.shape
        scale = D_OUT ** 0.5
        qkv = jnp.einsum('bnd,de->bne', x, W_qkv)
        q, k, v = jnp.split(qkv, 3, axis=-1)
        scores = jnp.einsum('bnd,bmd->bnm', q, k) / scale
        causal = jnp.triu(jnp.ones((N, N), dtype=bool), k=1)
        scores = jnp.where(causal, -jnp.inf, scores)
        attn = jax.nn.softmax(scores, axis=-1)
        return jnp.einsum('bnm,bmd->bnd', attn, v)

    def _L0_ffn_ref(x, router, experts_gate, experts_up, experts_down, shared_gate, shared_up, shared_down):
        import jax, jax.numpy as jnp
        import numpy as np
        TOP_K = 2
        NUM_EXPERTS = 8
        b, s, h = x.shape
        E = router.shape[1]
        shared_act = jax.nn.silu(jnp.einsum('bsh,hd->bsd', x, shared_gate))
        shared_up_out = jnp.einsum('bsh,hd->bsd', x, shared_up)
        shared_out = jnp.einsum('bsd,dh->bsh', shared_act * shared_up_out, shared_down)
        router_probs = jax.nn.softmax(jnp.einsum('bsh,he->bse', x, router), axis=-1)
        topk_probs, topk_idx = jax.lax.top_k(router_probs, TOP_K)
        coef = jnp.sum(jax.nn.one_hot(topk_idx, E, dtype=x.dtype) * topk_probs[..., None], axis=2)
        coef = coef.reshape(b * s, E)
        x_flat = x.reshape(b * s, h)
        gate = jnp.einsum('th,ehd->etd', x_flat, experts_gate)
        up = jnp.einsum('th,ehd->etd', x_flat, experts_up)
        expert_out = jnp.einsum('etd,edh->eth', jax.nn.silu(gate) * up, experts_down)
        routed = jnp.einsum('eth,te->th', expert_out, coef)
        return routed.reshape(b, s, h) + shared_out
    x = L0_attn_x
    x = x + _layernorm(_L0_attn_ref(_layernorm(x, axis=-1), L0_attn_W_qkv), axis=-1)
    x = x + _layernorm(_L0_ffn_ref(_layernorm(x, axis=-1), L0_ffn_router, L0_ffn_experts_gate, L0_ffn_experts_up, L0_ffn_experts_down, L0_ffn_shared_gate, L0_ffn_shared_up, L0_ffn_shared_down), axis=-1)
    return x

_drawn_inputs = setup_inputs


def setup_inputs(seed=0):
    import zlib

    import numpy as np

    out = dict(_drawn_inputs(seed))
    spreads = {}
    factors = {}
    for name, (base, spread) in spreads.items():
        noise = np.random.default_rng([zlib.crc32(name.encode()), seed]).standard_normal(out[name].shape)
        drawn = base * np.exp(spread * noise) if base else spread * noise
        out[name] = jnp.asarray(drawn.astype(out[name].dtype))
    for name, factor in factors.items():
        out[name] = (out[name] * factor).astype(out[name].dtype)
    return out
```

```python
from contextlib import ExitStack

import concourse.bass as bass
from concourse import mybir

F32 = mybir.dt.float32
F32R = mybir.dt.float32r
BF16 = mybir.dt.bfloat16
ALU = mybir.AluOpType
ACT = mybir.ActivationFunctionType
AX = mybir.AxisListType

P = 128
EPS = 1e-5
TOP_K = 2
MASKED = -1e38


class Batch:

    def __init__(self, i, shift=0):
        self.i, self.shift = i, shift

    def index(self):
        return self.i + self.shift if self.shift else self.i

    def count(self, per_batch, k):
        return self.i * per_batch + (self.shift * per_batch + k)

    def reaches(self, k):
        return k > 0 or not self.is_first()

    def is_first(self):
        return isinstance(self.i, int) and self.i + self.shift == 0


def layer_kernel(nc, x_dram, W_qkv, router, experts_gate, experts_up, experts_down,
                 shared_gate, shared_up, shared_down, out_dram):
    B, N, D = x_dram.shape
    E, _, DE = experts_gate.shape
    DS = shared_gate.shape[1]
    NT = N // P
    KB = D // P
    SU = DS // P
    NU = SU + E
    assert DE == P and KB == 2 and NT == 4 and D == 256 and SU == 2
    SCALE = float(D) ** -0.5
    SPREADS = 3
    spread_turns = [len(range(n, E, SPREADS)) for n in range(SPREADS)]
    order = list(range(NT - 1, -1, -1))
    width = [(q + 1) * P for q in range(NT)]
    start = [sum(width[:q]) for q in range(NT)]
    packed = sum(width)

    with ExitStack() as ctx:
        def sb(name, shape, dt=F32):
            return ctx.enter_context(nc.sbuf_tensor(name, shape, dt))

        def sem(name):
            return ctx.enter_context(nc.semaphore(name))

        score_w = [sb("score_w_hi", [P, KB, D], F32R), sb("score_w_lo", [P, KB, D], F32R)]
        value_w = [sb("value_w_hi", [P, KB, D], F32R), sb("value_w_lo", [P, KB, D], F32R)]
        router_w = sb("router_w", [P, KB, P], F32R)
        gate_w = [sb("gate_w_hi", [P, KB, NU, P], F32R), sb("gate_w_lo", [P, KB, NU, P], F32R)]
        up_w = [sb("up_w_hi", [P, KB, NU, P], F32R), sb("up_w_lo", [P, KB, NU, P], F32R)]
        down_w = [sb("down_w_hi", [P, NU, D], F32R), sb("down_w_lo", [P, NU, D], F32R)]

        ident = sb("ident", [P, P])
        ident_bf = sb("ident_bf", [P, P], BF16)
        causal_bf = sb("causal_bf", [P, P], BF16)
        earlier = sb("earlier", [P, E, E])
        neg_half = sb("neg_half", [P, NT])
        scratch = sb("scratch", [P, 2])

        x = sb("x", [P, NT, D])
        xn = sb("xn", [P, NT, D])
        xnT = [sb("xnT_hi", [P, KB, N], F32R), sb("xnT_lo", [P, KB, N], F32R)]
        qT = [sb("qT_hi", [P, KB, N], F32R), sb("qT_lo", [P, KB, N], F32R)]
        v = [sb("v_hi", [P, NT, D], F32R), sb("v_lo", [P, NT, D], F32R)]
        probs = sb("probs", [P, packed])
        probsT = [sb("probsT_hi", [P, packed], F32R), sb("probsT_lo", [P, packed], F32R)]
        neg_max = sb("neg_max", [P, NT])
        row_sum = sb("row_sum", [P, NT])
        sum_sq_eps = sb("sum_sq_eps", [P, NT])
        x1 = sb("x1", [P, NT, D + 1])
        ending = sb("ending", [P, NT * (2 * D + 1)])
        x1_ffn = ending[:, 0:NT * (D + 1)].rearrange("p (t d) -> p t d", t=NT)
        y_norm = ending[:, NT * (D + 1):].rearrange("p (t d) -> p t d", t=NT)
        h = sb("h", [P, NT, D])
        hT = [sb("hT_hi", [P, KB, N], F32R), sb("hT_lo", [P, KB, N], F32R)]
        stats = {n: sb(f"{n}_stats", [P, NT, 6]) for n in ("x", "o", "x1", "y")}
        moments = {n: sb(f"{n}_moments", [P, NT, 2]) for n in ("x", "o", "x1", "y")}
        var_eps = {n: sb(f"{n}_var_eps", [P, NT]) for n in ("x", "o", "x1", "y")}
        rstd = {n: sb(f"{n}_rstd", [P, NT]) for n in ("x", "o", "x1", "y")}

        logitsT = sb("logitsT", [P, N])
        logits_parts = sb("logits_parts", [P, NT, 2 * E])
        logits = sb("logits", [P, NT, E])
        logit_max = sb("logit_max", [P, NT])
        shifted = sb("shifted", [P, NT, E])
        exps = sb("exps", [P, NT, E])
        exp_sum = sb("exp_sum", [P, NT])
        exp_rec = sb("exp_rec", [P, NT])
        route_p = sb("route_p", [P, NT, E])
        greater = sb("greater", [P, NT, E, E])
        equal = sb("equal", [P, NT, E, E])
        rank = sb("rank", [P, NT, E])
        coef = sb("coef", [P, NT, P])
        coefT = logitsT
        spread = sb("spread", [P, SPREADS, N])

        middle = sb("middle", [P, 3, 2, N])
        silu_g, gated, act = middle[:, 0], middle[:, 1], middle[:, 2]
        actT = [sb("act_hi", [P, NU, N], F32R), sb("act_lo", [P, NU, N], F32R)]
        out_bias = sb("out_bias", [P, NT])
        stage = [ending[:, 0:KB * E * P], middle[:, :, :, :].rearrange("p k s n -> p (k s n)")[:, 0:KB * E * P]]

        F = [ctx.enter_context(nc.psum_tensor(f"ffn_bank{n}", [P, N], F32)) for n in range(4)]
        A = [ctx.enter_context(nc.psum_tensor(f"attn_bank{n}", [P, N], F32)) for n in range(4)]
        O_BANK = (1, 0)

        ident_set = sem("ident_set")
        masks_done = sem("masks_done")
        qkv_loaded, shared_loaded = sem("qkv_loaded"), sem("shared_loaded")
        gate_loaded, up_loaded, down_loaded = sem("gate_loaded"), sem("up_loaded"), sem("down_loaded")
        qkT_psum, qkT_done, m_psum, m_scaled = (sem("qkT_psum"), sem("qkT_done"), sem("m_psum"), sem("m_scaled"))
        hi_ready = sem("hi_ready")
        lo_ready = sem("lo_ready")
        ffn_lo_ready = sem("ffn_lo_ready")

        x_loaded = sem("x_loaded")
        x1_copied = sem("x1_copied")
        out_stored = sem("out_stored")

        ln_stats = {n: sem(f"{n}_stats_done") for n in ("x", "o", "x1")}
        ln_moments = {n: sem(f"{n}_moments_done") for n in ("x", "o", "x1")}
        ln_var = {n: sem(f"{n}_var_done") for n in ("x", "o", "x1")}
        ln_rstd = {n: sem(f"{n}_rstd_done") for n in ("x", "o", "x1")}
        xn_ready = sem("xn_ready")
        xnT_psum, xnT_hi, xnT_lo = sem("xnT_psum"), sem("xnT_hi_done"), sem("xnT_lo_done")
        qT_psum, qT_hi, qT_lo = sem("qT_psum"), sem("qT_hi_done"), sem("qT_lo_done")
        v_psum, v_hi, v_lo = sem("v_psum"), sem("v_hi_done"), sem("v_lo_done")
        scores_psum, max_done, exp_done = sem("scores_psum"), sem("max_done"), sem("exp_done")
        probsT_psum, probsT_hi, probsT_lo = sem("probsT_psum"), sem("probsT_hi_done"), sem("probsT_lo_done")
        o_psum = sem("o_psum")
        sum_sq_done = sem("sum_sq_done")
        x1_done = sem("x1_done")
        h_ready = sem("h_ready")
        hT_psum, hT_hi, hT_lo = sem("hT_psum"), sem("hT_hi_done"), sem("hT_lo_done")
        logitsT_psum, logitsT_done = sem("logitsT_psum"), sem("logitsT_done")
        logits_psum, logits_done, logits_summed = sem("logits_psum"), sem("logits_done"), sem("logits_summed")
        logit_max_done, shifted_done, exps_done = sem("logit_max_done"), sem("shifted_done"), sem("exps_done")
        exp_sum_done, exp_rec_done, route_p_done = sem("exp_sum_done"), sem("exp_rec_done"), sem("route_p_done")
        equal_done, ties_done, beaten_done, rank_done = (
            sem("equal_done"), sem("ties_done"), sem("beaten_done"), sem("rank_done"))
        coef_done = sem("coef_done")
        coef_stored = sem("coef_stored")
        coef_spread = [sem(f"coef_spread{n}") for n in range(SPREADS)]
        coefT_psum, coefT_done = sem("coefT_psum"), sem("coefT_done")

        gate_psum, up_psum = sem("gate_psum"), sem("up_psum")
        silu_done, gated_done, act_done = sem("silu_done"), sem("gated_done"), sem("act_done")
        act_hi_done, act_lo_done = sem("act_hi_done"), sem("act_lo_done")
        y_psum, y_stats_done, y_moments_done, y_var_done, y_rstd_done, y_bias_done, y_norm_done, y_added = (
            sem("y_psum"), sem("y_stats_done"), sem("y_moments_done"), sem("y_var_done"),
            sem("y_rstd_done"), sem("y_bias_done"), sem("y_norm_done"), sem("y_added"))

        HI, LO = 0, 1
        PASSES = ((HI, HI), (HI, LO), (LO, HI))

        def f32(ap):
            return ap.bitcast(F32)

        shared_n = KB * DS
        qkv_st = stage[0][:, 0:KB * 3 * D].rearrange("p (b n) -> p b n", b=KB)
        sh_gate = stage[1][:, 0:shared_n].rearrange("p (b u d) -> p b u d", b=KB, u=SU)
        sh_up = stage[1][:, shared_n:2 * shared_n].rearrange("p (b u d) -> p b u d", b=KB, u=SU)
        sh_down = stage[1][:, 2 * shared_n:2 * shared_n + SU * D].rearrange("p (u n) -> p u n", u=SU)
        r_st = stage[1][:, 2 * shared_n + SU * D:2 * shared_n + SU * D + KB * E].rearrange("p (b e) -> p b e", b=KB)
        ex_gate = stage[0].rearrange("p (b e d) -> p b e d", b=KB, e=E)
        ex_up = stage[1].rearrange("p (b e d) -> p b e d", b=KB, e=E)
        ex_down = stage[0].rearrange("p (e n) -> p e n", e=E)

        coef_dram = nc.dram_tensor("coef_rows", (E, N), F32).ap()

        block = ctx.enter_context(nc.Block())

        @block.sync
        def _(sp):
            def load_x(b):
                if not b.is_first():
                    sp.wait_ge(x1_done, b.count(2, 0))
                sp.dma_start(x[:, :, :], x_dram[b.index()].rearrange("(t p) d -> p t d", p=P)).then_inc(x_loaded, 16)

            def spread_coef(b):
                sp.wait_ge(coefT_done, b.count(1, 1))
                sp.dma_start(coef_dram, coefT[0:E, :]).then_inc(coef_stored, 16)
                sp.wait_ge(coef_stored, b.count(16, 16))
                for e in range(E):
                    n, turn = e % SPREADS, e // SPREADS
                    if turn:
                        sp.wait_ge(act_done, b.count(NU, SU + e - SPREADS + 1))
                    sp.dma_start(spread[:, n, :], coef_dram[e:e + 1, :].to_broadcast([P, N])) \
                        .then_inc(coef_spread[n], 16)

            def copy_x1(b):
                sp.wait_ge(x1_done, b.count(2, 2))
                if not b.is_first():
                    sp.wait_ge(y_added, b.count(NT, 0))
                sp.dma_start(x1_ffn[:, :, :], x1[:, :, :]).then_inc(x1_copied, 16)

            def store(b):
                sp.wait_ge(y_added, b.count(NT, NT))
                sp.dma_start(out_dram[b.index()].rearrange("(t p) d -> p t d", p=P), y_norm[:, :, :]) \
                    .then_inc(out_stored, 16)

            sp.dma_start(qkv_st, W_qkv.rearrange("(b p) n -> p b n", p=P)).then_inc(qkv_loaded, 16)
            load_x(Batch(0))
            sp.dma_start(sh_gate, shared_gate.rearrange("(b p) (u d) -> p b u d", p=P, u=SU)).then_inc(shared_loaded, 16)
            sp.dma_start(sh_up, shared_up.rearrange("(b p) (u d) -> p b u d", p=P, u=SU)).then_inc(shared_loaded, 16)
            sp.dma_start(sh_down, shared_down.rearrange("(u p) n -> p u n", p=P)).then_inc(shared_loaded, 16)
            sp.dma_start(r_st, router.rearrange("(b p) e -> p b e", p=P)).then_inc(shared_loaded, 16)
            sp.wait_ge(lo_ready, 1)
            sp.wait_ge(qkT_psum, 1)
            for b in range(KB):
                sp.dma_start(ex_gate[:, b], experts_gate[:, b * P:(b + 1) * P, :].rearrange("e p d -> p e d")) \
                    .then_inc(gate_loaded, 16)
            sp.wait_ge(ffn_lo_ready, 4)
            for b in range(KB):
                sp.dma_start(ex_up[:, b], experts_up[:, b * P:(b + 1) * P, :].rearrange("e p d -> p e d")) \
                    .then_inc(up_loaded, 16)
            sp.wait_ge(ffn_lo_ready, 5)
            sp.dma_start(ex_down, experts_down.rearrange("e p n -> p e n")).then_inc(down_loaded, 16)

            load_x(Batch(0, 1))
            sp.wait_ge(ffn_lo_ready, 7)
            copy_x1(Batch(0))

            def iteration(i, attn):
                spread_coef(Batch(i))
                if attn == 2:
                    load_x(Batch(i, 2))
                store(Batch(i))
                if attn:
                    copy_x1(Batch(i, 1))

            iteration(0, 2)
            with sp.Fori(1, B - 2) as i:
                iteration(i, 2)
            iteration(B - 2, 1)
            iteration(B - 1, 0)
            sp.wait_ge(out_stored, 16 * B)

        @block.tensor
        def _(pe):
            def split_matmul(out, pairs, first=True):
                for n, (lhs, rhs) in enumerate(pairs):
                    for p, (a, b) in enumerate(PASSES):
                        mm = nc.tensor.matmul(out, lhs[a], rhs[b], start=first and n == 0 and p == 0,
                                              stop=n == len(pairs) - 1 and p == len(PASSES) - 1)
                return mm

            def both(t, *key):
                return [t[HI][key], t[LO][key]]

            def transpose_xn(b):
                pe.wait_ge(xn_ready, b.count(1, 1))
                for k in range(KB):
                    for t in range(NT):
                        mm = nc.tensor.transpose(A[k][:, t * P:(t + 1) * P], xn[:, t, k * P:(k + 1) * P], ident[:, :])
                    mm.then_inc(xnT_psum, 1)

            def project_q(b):
                pe.wait_ge(xnT_lo, b.count(KB, KB))
                if b.is_first():
                    pe.wait_ge(lo_ready, 2)
                for m in range(KB):
                    if m == 0 and not b.is_first():
                        pe.wait_ge(logits_done, b.count(1, 0))
                    mm = split_matmul(A[2 if m == 0 else 0][:, :],
                                      [(both(score_w, slice(None), k, slice(m * P, (m + 1) * P)),
                                        both(xnT, slice(None), k, slice(None))) for k in range(KB)])
                    mm.then_inc(qT_psum, 1)

            def project_v(b):
                for pair in range(2):
                    if pair == 1:
                        pe.wait_ge(qT_lo, b.count(KB, 1))
                    for t in (2 * pair, 2 * pair + 1):
                        mm = split_matmul(A[1 + pair][:, t % 2 * D:(t % 2 + 1) * D],
                                          [(both(xnT, slice(None), k, slice(t * P, (t + 1) * P)),
                                            both(value_w, slice(None), k, slice(None))) for k in range(KB)])
                    mm.then_inc(v_psum, 1)

            def scores(b, n):
                q = order[n]
                if n == 0:
                    pe.wait_ge(qT_lo, b.count(KB, 2))
                elif n < 3:
                    pe.wait_ge(v_lo, b.count(2, n))
                elif not b.is_first():
                    pe.wait_ge(coefT_done, b.count(1, 0))
                out = A[n]
                for m in range(KB):
                    for p, (s, r) in enumerate(PASSES):
                        nc.tensor.matmul(out[:, 0:width[q]], qT[s][:, m, q * P:(q + 1) * P],
                                         xnT[r][:, m, 0:width[q]], start=m == 0 and p == 0,
                                         stop=m == KB - 1 and p == len(PASSES) - 1)
                nc.tensor.matmul(out[:, q * P:(q + 1) * P], ident_bf[:, :], causal_bf[:, :],
                                 start=False, stop=True, skip_group_check=True).then_inc(scores_psum, 1)

            def transpose_probs(b, n):
                q = order[n]
                pe.wait_ge(exp_done, b.count(NT, n + 1))
                for j in range(q + 1):
                    at = start[q] + j * P
                    mm = nc.tensor.transpose(A[n][:, j * P:(j + 1) * P], probs[:, at:at + P], ident[:, :])
                mm.then_inc(probsT_psum, 1)

            def weigh_values(b, pair):
                pe.wait_ge(probsT_lo, b.count(NT, 2 * pair + 2))
                for n in (2 * pair, 2 * pair + 1):
                    q = order[n]
                    mm = split_matmul(A[O_BANK[pair]][:, n % 2 * D:(n % 2 + 1) * D],
                                      [(both(probsT, slice(None), slice(start[q] + j * P, start[q] + (j + 1) * P)),
                                        both(v, slice(None), j, slice(None))) for j in range(q + 1)])
                mm.then_inc(o_psum, 1)

            def transpose_h(b):
                pe.wait_ge(h_ready, b.count(1, 1))
                for k in range(KB):
                    for t in range(NT):
                        mm = nc.tensor.transpose(A[1 + k][:, t * P:(t + 1) * P], h[:, t, k * P:(k + 1) * P], ident[:, :])
                    mm.then_inc(hT_psum, 1)

            def route(b):
                pe.wait_ge(hT_lo, b.count(KB, KB))
                if b.is_first():
                    pe.wait_ge(ffn_lo_ready, 4)
                for k in range(KB):
                    for half in (LO, HI):
                        mm = nc.tensor.matmul(A[0][:, :], router_w[:, k, :], hT[half][:, k, :],
                                              start=k == 0 and half == LO, stop=k == KB - 1 and half == HI)
                mm.then_inc(logitsT_psum, 1)

            def transpose_logits(b):
                pe.wait_ge(logitsT_done, b.count(1, 1))
                for t in range(NT):
                    mm = nc.tensor.transpose(A[2][:, t * P:(t + 1) * P], logitsT[:, t * P:(t + 1) * P], ident[:, :])
                mm.then_inc(logits_psum, 1)

            def gate_up(b, u):
                g, up = F[2 * (u % 2)], F[2 * (u % 2) + 1]
                if u >= 2:
                    pe.wait_ge(silu_done, b.count(NU, u - 1))
                elif not b.is_first():
                    pe.wait_ge(y_norm_done, b.count(NT, 2 * u + 1 - NT))
                split_matmul(g[:, :], [(both(gate_w, slice(None), k, u, slice(None)),
                                        both(hT, slice(None), k, slice(None))) for k in range(KB)]) \
                    .then_inc(gate_psum, 1)
                if u >= 2 + SU:
                    pe.wait_ge(gated_done, b.count(E, u - 1 - SU))
                elif u >= 2:
                    pe.wait_ge(act_done, b.count(NU, u - 1))
                elif not b.is_first():
                    pe.wait_ge(y_norm_done, b.count(NT, 2 * u + 2 - NT))
                split_matmul(up[:, :], [(both(up_w, slice(None), k, u, slice(None)),
                                         both(hT, slice(None), k, slice(None))) for k in range(KB)]) \
                    .then_inc(up_psum, 1)

            def transpose_coef(b):
                pe.wait_ge(coef_done, b.count(1, 1))
                for t in range(NT):
                    mm = nc.tensor.transpose(A[3][:, t * P:(t + 1) * P], coef[:, t, :], ident[:, :])
                mm.then_inc(coefT_psum, 1)

            def down(b, t, units):
                for u in units:
                    for p, (s, r) in enumerate(PASSES):
                        mm = nc.tensor.matmul(F[t][:, 0:D], actT[s][:, u, t * P:(t + 1) * P], down_w[r][:, u, :],
                                              start=u == 0 and p == 0, stop=u == NU - 1 and p == len(PASSES) - 1)
                return mm

            def down_first_two(b):
                early = range(NU - 1)
                pe.wait_ge(act_lo_done, b.count(NU, NU - 2))
                pe.wait_ge(silu_done, b.count(NU, NU - 1))
                down(b, 0, early[:-1])
                pe.wait_ge(gated_done, b.count(E, E - 1))
                down(b, 1, early[:-1])
                pe.wait_ge(act_lo_done, b.count(NU, NU - 1))
                down(b, 0, early[-1:])
                down(b, 1, early[-1:])
                pe.wait_ge(act_lo_done, b.count(NU, NU))
                for t in range(2):
                    down(b, t, [NU - 1]).then_inc(y_psum, 1)

            pe.wait_ge(ident_set, 2)
            pe.wait_ge(qkv_loaded, 16)
            for side in range(2):
                for d in range(KB):
                    for k in range(KB):
                        mm = nc.tensor.transpose(F[side][:, d * D + k * P:d * D + (k + 1) * P],
                                                 qkv_st[:, k, side * D + d * P:side * D + (d + 1) * P], ident[:, :])
            mm.then_inc(qkT_psum, 1)
            pe.wait_ge(qkT_done, 2)
            hf = h[:, :, :].rearrange("p t d -> p (t d)")
            for i in range(KB):
                for d in range(KB):
                    mm = nc.tensor.matmul(F[2][:, i * D:(i + 1) * D], hf[:, d * D + i * P:d * D + (i + 1) * P],
                                          hf[:, N + d * D:N + (d + 1) * D], start=d == 0, stop=d == KB - 1)
            mm.then_inc(m_psum, 1)

            def attention_alone(b):
                transpose_xn(b)
                project_q(b)
                project_v(b)
                pe.wait_ge(masks_done, 1)
                for n in range(NT):
                    scores(b, n)
                for n in range(NT):
                    transpose_probs(b, n)
                weigh_values(b, 0)
                weigh_values(b, 1)
                transpose_h(b)
                route(b)
                transpose_logits(b)

            def iteration(i, attn):
                b, c = Batch(i), Batch(i, 1)
                for u in range(NU):
                    gate_up(b, u)
                    if attn and u == 1:
                        project_q(c)
                    if u == 1:
                        transpose_coef(b)
                    if attn and u == 2:
                        project_v(c)
                    if attn and u == 3:
                        scores(c, 0)
                        scores(c, 1)
                    if attn and u == 4:
                        scores(c, 2)
                        scores(c, 3)
                    if attn and u == 5:
                        transpose_probs(c, 0)
                        transpose_probs(c, 1)
                    if attn and u == 6:
                        transpose_probs(c, 2)
                        transpose_probs(c, 3)
                    if attn and u == 7:
                        weigh_values(c, 0)
                    if attn and u == 8:
                        weigh_values(c, 1)
                if b.is_first():
                    pe.wait_ge(ffn_lo_ready, 7)
                down_first_two(b)
                down(b, 2, range(NU // 2))
                if attn:
                    transpose_h(c)
                down(b, 2, range(NU // 2, NU)).then_inc(y_psum, 1)
                down(b, 3, range(3))
                if attn:
                    route(c)
                down(b, 3, range(3, NU)).then_inc(y_psum, 1)
                if attn:
                    transpose_logits(c)
                if attn == 2:
                    transpose_xn(Batch(i, 2))

            attention_alone(Batch(0))
            pe.wait_ge(ffn_lo_ready, 6)
            transpose_xn(Batch(0, 1))
            iteration(0, 2)
            with pe.Fori(1, B - 2) as i:
                iteration(i, 2)
            iteration(B - 2, 1)
            iteration(B - 1, 0)

        @block.scalar
        def _(act_e):
            def xnT_his(b):
                for k in range(KB):
                    act_e.wait_ge(xnT_psum, b.count(KB, k + 1))
                    nc.scalar.activation(xnT[HI][:, k, :], A[k][:, :], ACT.Copy) \
                        .then_inc(xnT_hi, 1)

            def qT_his(b):
                for m in range(KB):
                    act_e.wait_ge(qT_psum, b.count(KB, m + 1))
                    nc.scalar.activation(qT[HI][:, m, :], A[2 if m == 0 else 0][:, :], ACT.Copy) \
                        .then_inc(qT_hi, 1)

            def v_his(b):
                for pair in range(2):
                    act_e.wait_ge(v_psum, b.count(2, pair + 1))
                    nc.scalar.activation(v[HI][:, 2 * pair:2 * pair + 2, :].rearrange("p t d -> p (t d)"), A[1 + pair][:, :], ACT.Copy) \
                        .then_inc(v_hi, 1)

            def exp(b, n):
                q = order[n]
                act_e.wait_ge(max_done, b.count(NT, n + 1))
                nc.scalar.activation(probs[:, start[q]:start[q] + width[q]], A[n][:, 0:width[q]], ACT.Exp,
                                     bias=neg_max[:, q:q + 1], accum_out=row_sum[:, q:q + 1]).then_inc(exp_done, 1)

            def probsT_his(b, n):
                q = order[n]
                act_e.wait_ge(probsT_psum, b.count(NT, n + 1))
                nc.scalar.activation(probsT[HI][:, start[q]:start[q] + width[q]], A[n][:, 0:width[q]], ACT.Copy) \
                    .then_inc(probsT_hi, 1)

            def hT_his(b):
                for k in range(KB):
                    act_e.wait_ge(hT_psum, b.count(KB, k + 1))
                    nc.scalar.activation(hT[HI][:, k, :], A[1 + k][:, :], ACT.Copy) \
                        .then_inc(hT_hi, 1)

            def logitsT_copy(b):
                act_e.wait_ge(logitsT_psum, b.count(1, 1))
                if not b.is_first():
                    act_e.wait_ge(coef_stored, b.count(16, 0))
                nc.scalar.activation(logitsT[:, :], A[0][:, :], ACT.Copy).then_inc(logitsT_done, 1)

            def router_exp(b):
                act_e.wait_ge(shifted_done, b.count(1, 1))
                nc.scalar.activation(exps[:, :, :], shifted[:, :, :], ACT.Exp).then_inc(exps_done, 1)

            def coefT_copy(b):
                act_e.wait_ge(coefT_psum, b.count(1, 1))
                nc.scalar.activation(coefT[0:E, :], A[3][0:E, :], ACT.Copy).then_inc(coefT_done, 1)

            def silu(b, u):
                act_e.wait_ge(gate_psum, b.count(NU, u + 1))
                if u >= 2 + SU:
                    act_e.wait_ge(gated_done, b.count(E, u - 1 - SU))
                elif u >= 2:
                    act_e.wait_ge(act_done, b.count(NU, u - 1))
                nc.scalar.activation(silu_g[:, u % 2, :], F[2 * (u % 2)][:, :], ACT.Silu).then_inc(silu_done, 1)

            def act_hi(b, u):
                act_e.wait_ge(act_done, b.count(NU, u + 1))
                nc.scalar.activation(actT[HI][:, u, :], act[:, u % 2, :], ACT.Copy) \
                    .then_inc(act_hi_done, 1)

            def normalise_y(b, t):
                act_e.wait_ge(y_bias_done, b.count(NT, t + 1))
                if not b.is_first():
                    act_e.wait_ge(out_stored, b.count(16, 0))
                nc.scalar.activation(y_norm[:, t, :], F[t][:, 0:D], ACT.Identity, bias=out_bias[:, t:t + 1],
                                     scale=rstd["y"][:, t:t + 1]).then_inc(y_norm_done, 1)

            def attention_alone(b):
                xnT_his(b)
                qT_his(b)
                v_his(b)
                for n in range(NT):
                    exp(b, n)
                for n in range(NT):
                    probsT_his(b, n)
                hT_his(b)
                logitsT_copy(b)
                xnT_his(Batch(0, 1))
                router_exp(b)

            def iteration(i, attn):
                b, c = Batch(i), Batch(i, 1)
                for u in range(NU):
                    silu(b, u)
                    if u >= 1:
                        act_hi(b, u - 1)
                    if attn and u == 1:
                        qT_his(c)
                    if u == 1:
                        coefT_copy(b)
                    if attn and u == 2:
                        v_his(c)
                    if attn and u == 4:
                        for n in range(NT):
                            exp(c, n)
                    if attn and u == 5:
                        probsT_his(c, 0)
                        probsT_his(c, 1)
                    if attn and u == 6:
                        probsT_his(c, 2)
                        probsT_his(c, 3)
                act_hi(b, NU - 1)
                if attn:
                    hT_his(c)
                    logitsT_copy(c)
                normalise_y(b, 0)
                normalise_y(b, 1)
                normalise_y(b, 2)
                if attn == 2:
                    xnT_his(Batch(i, 2))
                normalise_y(b, 3)
                if attn:
                    router_exp(c)

            hf = h[:, :, :].rearrange("p t d -> p (t d)")
            act_e.wait_ge(qkT_psum, 1)
            for side in range(2):
                nc.scalar.activation(hf[:, side * N:(side + 1) * N], F[side][:, :], ACT.Copy).then_inc(qkT_done, 1)
            attention_alone(Batch(0))
            iteration(0, 2)
            with act_e.Fori(1, B - 2) as i:
                iteration(i, 2)
            iteration(B - 2, 1)
            iteration(B - 1, 0)

        @block.vector
        def _(dve):
            def moments_of(name, b, sources):
                for t in range(NT):
                    ins = nc.vector.bn_stats(stats[name][:, t, :], sources[t])
                ins.then_inc(ln_stats[name], 1)
                finish_moments(name, b)

            def finish_moments(name, b):
                dve.wait_ge(ln_stats[name], b.count(1, 1))
                nc.vector.memset(scratch[:, 0:1], 0.0)
                for t in range(NT):
                    ins = nc.vector.bn_aggr(moments[name][:, t, :], stats[name][:, t, :])
                ins.then_inc(ln_moments[name], 1)
                dve.wait_ge(ln_moments[name], b.count(1, 1))
                if name == "o":
                    dve.wait_ge(sum_sq_done, b.count(1, 1))
                    nc.vector.tensor_tensor(var_eps[name][:, :], moments[name][:, :, 1], sum_sq_eps[:, :], ALU.add) \
                        .then_inc(ln_var[name], 1)
                else:
                    nc.vector.tensor_scalar(var_eps[name][:, :], moments[name][:, :, 1], EPS, None, ALU.add) \
                        .then_inc(ln_var[name], 1)

            def normalise(name, b, dst, src, sem_out):
                dve.wait_ge(ln_rstd[name], b.count(1, 1))
                for t in range(NT):
                    ins = nc.vector.tensor_scalar(dst[:, t, :], src(t), moments[name][:, t, 0:1],
                                                  rstd[name][:, t:t + 1], ALU.subtract, ALU.mult)
                ins.then_inc(sem_out, 1)

            def norm_x_stats(b):
                dve.wait_ge(x_loaded, b.count(16, 16))
                moments_of("x", b, [x[:, t, :] for t in range(NT)])

            def norm_x(b):
                if not b.is_first():
                    dve.wait_ge(xnT_psum, b.count(KB, 0))
                normalise("x", b, xn, lambda t: x[:, t, :], xn_ready)

            def xnT_los(b):
                for k in range(KB):
                    dve.wait_ge(xnT_hi, b.count(KB, k + 1))
                    nc.vector.tensor_tensor(xnT[LO][:, k, :], A[k][:, :], f32(xnT[HI][:, k, :]),
                                            ALU.subtract).then_inc(xnT_lo, 1)

            def qT_los(b):
                for m in range(KB):
                    dve.wait_ge(qT_hi, b.count(KB, m + 1))
                    nc.vector.tensor_tensor(qT[LO][:, m, :], A[2 if m == 0 else 0][:, :], f32(qT[HI][:, m, :]),
                                            ALU.subtract).then_inc(qT_lo, 1)

            def v_los(b):
                for pair in range(2):
                    at = lambda t: t[:, 2 * pair:2 * pair + 2, :].rearrange("p t d -> p (t d)")
                    dve.wait_ge(v_hi, b.count(2, pair + 1))
                    nc.vector.tensor_tensor(at(v[LO]), A[1 + pair][:, :], f32(at(v[HI])),
                                            ALU.subtract).then_inc(v_lo, 1)

            def row_max(b, n):
                q = order[n]
                dve.wait_ge(scores_psum, b.count(NT, n + 1))
                nc.vector.tensor_reduce(neg_max[:, q:q + 1], A[n][:, 0:width[q]], AX.X, ALU.max, negate=True) \
                    .then_inc(max_done, 1)

            def probsT_los(b, n):
                q = order[n]
                at = slice(start[q], start[q] + width[q])
                dve.wait_ge(probsT_hi, b.count(NT, n + 1))
                nc.vector.tensor_tensor(probsT[LO][:, at], A[n][:, 0:width[q]], f32(probsT[HI][:, at]),
                                        ALU.subtract).then_inc(probsT_lo, 1)

            def o_of(q):
                n = order.index(q)
                return A[O_BANK[n // 2]][:, n % 2 * D:(n % 2 + 1) * D]

            def o_stats(b, pair):
                dve.wait_ge(o_psum, b.count(2, pair + 1))
                for n in (2 * pair, 2 * pair + 1):
                    ins = nc.vector.bn_stats(stats["o"][:, order[n], :], o_of(order[n]))
                if pair == 0:
                    nc.vector.scalar_tensor_tensor(out=sum_sq_eps[:, :], in0=row_sum[:, :], scalar=EPS,
                                                   in1=row_sum[:, :], op0=ALU.mult, op1=ALU.mult) \
                        .then_inc(sum_sq_done, 1)
                else:
                    ins.then_inc(ln_stats["o"], 1)

            def make_x1(b):
                dve.wait_ge(ln_rstd["o"], b.count(1, 1))
                if not b.is_first():
                    dve.wait_ge(x1_copied, b.count(16, 0))
                nc.vector.scalar_tensor_tensor(out=x1[:, :, D], in0=moments["o"][:, :, 0], scalar=-1.0,
                                               in1=rstd["o"][:, :], op0=ALU.mult, op1=ALU.mult)
                for pair in range(2):
                    for n in (2 * pair, 2 * pair + 1):
                        q = order[n]
                        ins = nc.vector.scalar_tensor_tensor(out=x1[:, q, 0:D], in0=o_of(q), scalar=rstd["o"][:, q:q + 1],
                                                             in1=x[:, q, :], op0=ALU.mult, op1=ALU.add)
                    ins.then_inc(x1_done, 1)

            def x1_stats(b):
                dve.wait_ge(x1_done, b.count(2, 2))
                moments_of("x1", b, [x1[:, t, 0:D] for t in range(NT)])

            def norm_x1(b):
                normalise("x1", b, h, lambda t: x1[:, t, 0:D], h_ready)

            def hT_los(b):
                for k in range(KB):
                    dve.wait_ge(hT_hi, b.count(KB, k + 1))
                    nc.vector.tensor_tensor(hT[LO][:, k, :], A[1 + k][:, :], f32(hT[HI][:, k, :]),
                                            ALU.subtract).then_inc(hT_lo, 1)

            def bcast(ap, shape, axis):
                return ap.unsqueeze(axis).to_broadcast(shape)

            def route_first(b):
                dve.wait_ge(logits_psum, b.count(1, 1))
                nc.vector.tensor_copy(logits_parts[:, :, :], A[2][:, :].rearrange("p (t k) -> p t k", t=NT)[:, :, 0:2 * E]) \
                    .then_inc(logits_done, 1)
                dve.wait_ge(logits_done, b.count(1, 1))
                nc.vector.tensor_tensor(logits[:, :, :], logits_parts[:, :, 0:E], logits_parts[:, :, E:2 * E], ALU.add) \
                    .then_inc(logits_summed, 1)
                dve.wait_ge(logits_summed, b.count(1, 1))
                nc.vector.tensor_reduce(logit_max[:, :], logits[:, :, :], AX.X, ALU.max).then_inc(logit_max_done, 1)
                dve.wait_ge(logit_max_done, b.count(1, 1))
                nc.vector.tensor_tensor(shifted[:, :, :], logits[:, :, :], bcast(logit_max[:, :], [P, NT, E], 2),
                                        ALU.subtract).then_inc(shifted_done, 1)

            def route_rank(b):
                of_j = bcast(logits[:, :, :], [P, NT, E, E], 2)
                of_e = bcast(logits[:, :, :], [P, NT, E, E], 3)
                nc.vector.tensor_tensor(equal[:, :, :, :], of_j, of_e, ALU.is_equal).then_inc(equal_done, 1)
                nc.vector.tensor_tensor(greater[:, :, :, :], of_j, of_e, ALU.is_gt)
                dve.wait_ge(equal_done, b.count(1, 1))
                nc.vector.tensor_tensor(equal[:, :, :, :], equal[:, :, :, :],
                                        bcast(earlier[:, :, :], [P, NT, E, E], 1), ALU.mult).then_inc(ties_done, 1)
                dve.wait_ge(ties_done, b.count(1, 1))
                nc.vector.tensor_tensor(greater[:, :, :, :], greater[:, :, :, :], equal[:, :, :, :], ALU.add) \
                    .then_inc(beaten_done, 1)
                dve.wait_ge(beaten_done, b.count(1, 1))
                nc.vector.tensor_reduce(rank[:, :, :], greater[:, :, :, :], AX.X, ALU.add).then_inc(rank_done, 1)

            def route_last(b):
                dve.wait_ge(exps_done, b.count(1, 1))
                nc.vector.tensor_reduce(exp_sum[:, :], exps[:, :, :], AX.X, ALU.add).then_inc(exp_sum_done, 1)
                dve.wait_ge(exp_sum_done, b.count(1, 1))
                nc.vector.reciprocal(exp_rec[:, :], exp_sum[:, :]).then_inc(exp_rec_done, 1)
                dve.wait_ge(exp_rec_done, b.count(1, 1))
                nc.vector.tensor_tensor(route_p[:, :, :], exps[:, :, :], bcast(exp_rec[:, :], [P, NT, E], 2), ALU.mult) \
                    .then_inc(route_p_done, 1)
                dve.wait_ge(route_p_done, b.count(1, 1))
                if not b.is_first():
                    dve.wait_ge(coefT_psum, b.count(1, 0))
                nc.vector.scalar_tensor_tensor(out=coef[:, :, 0:E], in0=rank[:, :, :], scalar=TOP_K - 0.5,
                                               in1=route_p[:, :, :], op0=ALU.is_lt, op1=ALU.mult) \
                    .then_inc(coef_done, 1)

            def hidden(b, u):
                dve.wait_ge(silu_done, b.count(NU, u + 1))
                dve.wait_ge(up_psum, b.count(NU, u + 1))
                up = F[2 * (u % 2) + 1]
                if u < SU:
                    if b.reaches(u - 1):
                        dve.wait_ge(act_lo_done, b.count(NU, u - 1))
                    nc.vector.tensor_tensor(act[:, u % 2, :], up[:, :], silu_g[:, u % 2, :], ALU.mult) \
                        .then_inc(act_done, 1)
                    return
                nc.vector.tensor_tensor(gated[:, u % 2, :], up[:, :], silu_g[:, u % 2, :], ALU.mult) \
                    .then_inc(gated_done, 1)
                dve.wait_ge(gated_done, b.count(E, u - SU + 1))
                n, turn = (u - SU) % SPREADS, (u - SU) // SPREADS
                dve.wait_ge(coef_spread[n], b.count(16 * spread_turns[n], 16 * (turn + 1)))
                if b.reaches(u - 1):
                    dve.wait_ge(act_lo_done, b.count(NU, u - 1))
                nc.vector.tensor_tensor(act[:, u % 2, :], spread[:, n, :], gated[:, u % 2, :], ALU.mult).then_inc(act_done, 1)

            def y_moments(b, t):
                dve.wait_ge(y_psum, b.count(NT, t + 1))
                nc.vector.bn_stats(stats["y"][:, t, :], F[t][:, 0:D]).then_inc(y_stats_done, 1)
                dve.wait_ge(y_stats_done, b.count(NT, t + 1))
                nc.vector.memset(scratch[:, 1:2], 0.0)
                nc.vector.bn_aggr(moments["y"][:, t, :], stats["y"][:, t, :]).then_inc(y_moments_done, 1)
                dve.wait_ge(y_moments_done, b.count(NT, t + 1))
                nc.vector.tensor_scalar(var_eps["y"][:, t:t + 1], moments["y"][:, t, 1:2], EPS, None, ALU.add) \
                    .then_inc(y_var_done, 1)

            def y_bias(b, t):
                dve.wait_ge(y_rstd_done, b.count(NT, t + 1))
                if t == 0:
                    dve.wait_ge(x1_copied, b.count(16, 16))
                nc.vector.scalar_tensor_tensor(out=out_bias[:, t:t + 1], in0=moments["y"][:, t, 0:1],
                                               scalar=rstd["y"][:, t:t + 1], in1=x1_ffn[:, t, D:D + 1],
                                               op0=ALU.mult, op1=ALU.subtract, reverse1=True).then_inc(y_bias_done, 1)

            def split(n, dst, src, sem_out=lo_ready):
                nc.vector.tensor_copy(dst[HI], src).then_inc(hi_ready, 1)
                if sem_out is not None:
                    dve.wait_ge(hi_ready, n)
                    nc.vector.tensor_tensor(dst[LO], src, f32(dst[HI]), ALU.subtract).then_inc(sem_out, 1)

            norm_x_stats(Batch(0))
            dve.wait_ge(qkv_loaded, 16)
            split(1, [value_w[HI][:, :, :], value_w[LO][:, :, :]], qkv_st[:, :, 2 * D:3 * D])
            norm_x(Batch(0))
            dve.wait_ge(m_psum, 1)
            m_sc = probs[:, 0:KB * D].rearrange("p (b d) -> p b d", b=KB)
            nc.vector.tensor_scalar(m_sc, F[2][:, :].rearrange("p (b d) -> p b d", b=KB), SCALE, None, ALU.mult) \
                .then_inc(m_scaled, 1)
            dve.wait_ge(m_scaled, 1)
            split(2, [score_w[HI][:, :, :], score_w[LO][:, :, :]], m_sc)
            xnT_los(Batch(0))
            nc.vector.memset(coef[:, :, :], 0.0)
            nc.vector.memset(f32(router_w[:, :, :]), 0.0).then_inc(lo_ready, 1)
            dve.wait_ge(lo_ready, 3)
            dve.wait_ge(shared_loaded, 64)
            for n, (dst, src) in enumerate((
                    (gate_w[HI][:, :, 0:SU, :], sh_gate), (up_w[HI][:, :, 0:SU, :], sh_up),
                    (down_w[HI][:, 0:SU, :], sh_down), (router_w[:, :, 0:E], r_st))):
                nc.vector.tensor_copy(dst, src).then_inc(hi_ready, 1)

            def split_experts(n):
                loaded, value, dst, src = (
                    (gate_loaded, 32, gate_w[HI][:, :, SU:, :], ex_gate), (up_loaded, 32, up_w[HI][:, :, SU:, :], ex_up),
                    (down_loaded, 16, down_w[HI][:, SU:, :], ex_down))[n]
                dve.wait_ge(loaded, value)
                nc.vector.tensor_copy(dst, src).then_inc(hi_ready, 1)

            def attention_alone(b):
                qT_los(b)
                split_experts(0)
                v_los(b)
                for n in range(NT):
                    row_max(b, n)
                split_experts(1)
                for n in range(NT):
                    probsT_los(b, n)
                o_stats(b, 0)
                o_stats(b, 1)
                finish_moments("o", b)
                make_x1(b)
                x1_stats(b)
                norm_x1(b)
                hT_los(b)
                norm_x_stats(Batch(0, 1))
                route_first(b)
                norm_x(Batch(0, 1))
                route_rank(b)
                xnT_los(Batch(0, 1))
                route_last(b)
                split_experts(2)

            def iteration(i, attn):
                b, c, d = Batch(i), Batch(i, 1), Batch(i, 2)
                for u in range(NU):
                    hidden(b, u)
                    if attn and u == 1:
                        qT_los(c)
                    if attn and u == 2:
                        v_los(c)
                    if attn and u == 3:
                        row_max(c, 0)
                        row_max(c, 1)
                    if attn and u == 4:
                        row_max(c, 2)
                        row_max(c, 3)
                    if attn and u == 5:
                        probsT_los(c, 0)
                        probsT_los(c, 1)
                    if attn and u == 6:
                        probsT_los(c, 2)
                        probsT_los(c, 3)
                    if attn and u == 7:
                        o_stats(c, 0)
                    if attn and u == 8:
                        o_stats(c, 1)
                        finish_moments("o", c)
                if attn:
                    make_x1(c)
                    x1_stats(c)
                    norm_x1(c)
                if attn == 2:
                    norm_x_stats(d)
                if attn:
                    hT_los(c)
                y_moments(b, 0)
                y_moments(b, 1)
                if attn == 2:
                    norm_x(d)
                y_bias(b, 0)
                y_bias(b, 1)
                y_moments(b, 2)
                y_bias(b, 2)
                y_moments(b, 3)
                if attn:
                    route_first(c)
                y_bias(b, 3)
                if attn == 2:
                    xnT_los(d)
                if attn:
                    route_rank(c)
                    route_last(c)

            attention_alone(Batch(0))
            iteration(0, 2)
            with dve.Fori(1, B - 2) as i:
                iteration(i, 2)
            iteration(B - 2, 1)
            iteration(B - 1, 0)

        @block.gpsimd
        def _(pool):
            def rstd_of(name, b):
                pool.wait_ge(ln_var[name], b.count(1, 1))
                nc.gpsimd.tensor_tensor(rstd[name][:, :], var_eps[name][:, :], neg_half[:, :], ALU.pow) \
                    .then_inc(ln_rstd[name], 1)

            def act_lo(b, u):
                pool.wait_ge(act_hi_done, b.count(NU, u + 1))
                nc.gpsimd.tensor_tensor(actT[LO][:, u, :], act[:, u % 2, :], f32(actT[HI][:, u, :]), ALU.subtract) \
                    .then_inc(act_lo_done, 1)

            def y_rstd(b, t):
                pool.wait_ge(y_var_done, b.count(NT, t + 1))
                nc.gpsimd.tensor_tensor(rstd["y"][:, t:t + 1], var_eps["y"][:, t:t + 1], neg_half[:, 0:1], ALU.pow) \
                    .then_inc(y_rstd_done, 1)

            def y_add(b, t):
                pool.wait_ge(y_norm_done, b.count(NT, t + 1))
                nc.gpsimd.tensor_tensor(y_norm[:, t, :], y_norm[:, t, :], x1_ffn[:, t, 0:D], ALU.add) \
                    .then_inc(y_added, 1)

            nc.gpsimd.memset(ident[:, :], 0.0).then_inc(ident_set, 1)
            pool.wait_ge(ident_set, 1)
            nc.gpsimd.affine_select(out=ident[:, :], in_=ident[:, :], compare_op=ALU.not_equal, fill=1.0, base=0,
                                    pattern=[[-1, P]], channel_multiplier=1).then_inc(ident_set, 1)
            nc.gpsimd.memset(neg_half[:, :], -0.5).then_inc(ident_set, 1)
            nc.gpsimd.memset(causal_bf[:, :], 0.0).then_inc(ident_set, 1)
            nc.gpsimd.memset(earlier[:, :, :], 1.0).then_inc(ident_set, 1)
            pool.wait_ge(ident_set, 5)
            nc.gpsimd.tensor_copy(ident_bf[:, :], ident[:, :])
            nc.gpsimd.affine_select(out=causal_bf[:, :], in_=causal_bf[:, :], compare_op=ALU.is_ge, fill=MASKED, base=0,
                                    pattern=[[-1, P]], channel_multiplier=1)
            nc.gpsimd.affine_select(out=earlier[:, :, :], in_=earlier[:, :, :], compare_op=ALU.is_gt, fill=0.0, base=0,
                                    pattern=[[1, E], [-1, E]], channel_multiplier=0).then_inc(masks_done, 1)

            def lo_half(n, dst, src, hi):
                pool.wait_ge(hi_ready, n)
                nc.gpsimd.tensor_tensor(dst, src, f32(hi), ALU.subtract).then_inc(ffn_lo_ready, 1)

            rstd_of("x", Batch(0))
            lo_half(3, gate_w[LO][:, :, 0:SU, :], sh_gate, gate_w[HI][:, :, 0:SU, :])
            lo_half(4, up_w[LO][:, :, 0:SU, :], sh_up, up_w[HI][:, :, 0:SU, :])
            lo_half(5, down_w[LO][:, 0:SU, :], sh_down, down_w[HI][:, 0:SU, :])
            lo_half(6, router_w[:, :, E:2 * E], r_st, router_w[:, :, 0:E])
            lo_half(7, gate_w[LO][:, :, SU:, :], ex_gate, gate_w[HI][:, :, SU:, :])
            rstd_of("o", Batch(0))
            rstd_of("x1", Batch(0))
            lo_half(8, up_w[LO][:, :, SU:, :], ex_up, up_w[HI][:, :, SU:, :])
            rstd_of("x", Batch(0, 1))
            lo_half(9, down_w[LO][:, SU:, :], ex_down, down_w[HI][:, SU:, :])

            def iteration(i, attn):
                b, c, d = Batch(i), Batch(i, 1), Batch(i, 2)
                for u in range(NU):
                    if u == NU - 2 and attn:
                        rstd_of("o", c)
                    act_lo(b, u)
                if attn:
                    rstd_of("x1", c)
                if attn == 2:
                    rstd_of("x", d)
                y_rstd(b, 0)
                y_rstd(b, 1)
                y_add(b, 0)
                y_add(b, 1)
                y_rstd(b, 2)
                y_add(b, 2)
                y_rstd(b, 3)
                y_add(b, 3)

            iteration(0, 2)
            with pool.Fori(1, B - 2) as i:
                iteration(i, 2)
            iteration(B - 2, 1)
            iteration(B - 1, 0)


_INS = ["L0_attn_x", "L0_attn_W_qkv", "L0_ffn_router", "L0_ffn_experts_gate", "L0_ffn_experts_up",
        "L0_ffn_experts_down", "L0_ffn_shared_gate", "L0_ffn_shared_up", "L0_ffn_shared_down"]


def kernel(**inputs):
    import numpy as np
    import concourse.bacc as bacc
    from concourse.bass_utils import run_bass_kernel_spmd

    nc = bacc.Bacc("TRN2", target_bir_lowering=False, num_devices=1)
    arrays, args = {}, []
    for name in _INS:
        a = np.ascontiguousarray(inputs[name])
        arrays[f"in_{name}"] = a
        args.append(nc.dram_tensor(f"in_{name}", a.shape, mybir.dt.from_np(a.dtype), kind="ExternalInput").ap())
    x_shape = inputs["L0_attn_x"].shape
    args.append(nc.dram_tensor("out_x", x_shape, F32, kind="ExternalOutput").ap())
    layer_kernel(nc, *args)
    r = run_bass_kernel_spmd(nc, [arrays], core_ids=[0])
    return r.results[0]["out_x"]
```

```python
from contextlib import ExitStack

import concourse.bass as bass
from concourse import mybir

F32 = mybir.dt.float32
F32R = mybir.dt.float32r
BF16 = mybir.dt.bfloat16
ALU = mybir.AluOpType
ACT = mybir.ActivationFunctionType
AX = mybir.AxisListType

P = 128
EPS = 1e-5
TOP_K = 2
MASKED = -1e38
SQUARE = 32


class Batch:

    def __init__(self, i, shift=0):
        self.i, self.shift = i, shift

    def index(self):
        return self.i + self.shift if self.shift else self.i

    def count(self, per_batch, k):
        return self.i * per_batch + (self.shift * per_batch + k)

    def reaches(self, k):
        return k > 0 or not self.is_first()

    def is_first(self):
        return self.is_number(0)

    def is_number(self, n):
        return isinstance(self.i, int) and self.i + self.shift == n


def layer_kernel(nc, x_dram, W_qkv, router, experts_gate, experts_up, experts_down,
                 shared_gate, shared_up, shared_down, out_dram):
    B, N, D = x_dram.shape
    E, _, DE = experts_gate.shape
    DS = shared_gate.shape[1]
    NT = N // P
    KB = D // P
    NB = N // SQUARE
    SU = DS // P
    NU = SU + E
    assert DE == P and KB == 2 and NT == 4 and D == 256 and SU == 2
    SCALE = float(D) ** -0.5
    SPREADS = 3
    spread_turns = [len(range(n, E, SPREADS)) for n in range(SPREADS)]
    order = list(range(NT - 1, -1, -1))
    width = [(q + 1) * P for q in range(NT)]
    start = [sum(width[:q]) for q in range(NT)]
    packed = sum(width)

    with ExitStack() as ctx:
        def sb(name, shape, dt=F32):
            return ctx.enter_context(nc.sbuf_tensor(name, shape, dt))

        def sem(name):
            return ctx.enter_context(nc.semaphore(name))

        score_w = [sb("score_w_hi", [P, KB, D], F32R), sb("score_w_lo", [P, KB, D], F32R)]
        value_w = [sb("value_w_hi", [P, KB, D], F32R), sb("value_w_lo", [P, KB, D], F32R)]
        router_w = sb("router_w", [P, KB, P], F32R)
        gate_w = [sb("gate_w_hi", [P, KB, NU, P], F32R), sb("gate_w_lo", [P, KB, NU, P], F32R)]
        up_w = [sb("up_w_hi", [P, KB, NU, P], F32R), sb("up_w_lo", [P, KB, NU, P], F32R)]
        down_w = [sb("down_w_hi", [P, NU, D], F32R), sb("down_w_lo", [P, NU, D], F32R)]

        ident = sb("ident", [P, P])
        causal = sb("causal", [P, P], BF16)
        preference = sb("preference", [SQUARE, E])
        neg_half = sb("neg_half", [P, NT])
        scratch = sb("scratch", [P, 2])

        x = sb("x", [P, NT, D])
        xn = sb("xn", [P, NT, D])
        xnT_both = sb("xnT", [P, 2, KB, N], F32R)
        xnT = [xnT_both[:, 0], xnT_both[:, 1]]
        qT = [sb("qT_hi", [P, KB, N], F32R), sb("qT_lo", [P, KB, N], F32R)]
        v = [sb("v_hi", [P, NT, D], F32R), sb("v_lo", [P, NT, D], F32R)]
        probs = sb("probs", [P, packed])
        probsT = [sb("probsT_hi", [P, packed], F32R), sb("probsT_lo", [P, packed], F32R)]
        neg_max = sb("neg_max", [P, NT])
        row_sum = sb("row_sum", [P, NT])
        scores_lo = probs[:, start[0]:start[0] + P]
        sum_sq_eps = sb("sum_sq_eps", [P, NT])
        x1 = sb("x1", [P, NT, D + 1])
        ending = sb("ending", [P, NT * (2 * D + 1)])
        x1_ffn = ending[:, 0:NT * (D + 1)].rearrange("p (t d) -> p t d", t=NT)
        y_norm = ending[:, NT * (D + 1):].rearrange("p (t d) -> p t d", t=NT)
        h = sb("h", [P, NT, D])
        hT = [sb("hT_hi", [P, KB, N], F32R), sb("hT_lo", [P, KB, N], F32R)]
        stats = {n: sb(f"{n}_stats", [P, NT, 6]) for n in ("x", "o", "x1", "y")}
        moments = {n: sb(f"{n}_moments", [P, NT, 2]) for n in ("x", "o", "x1", "y")}
        var_eps = {n: sb(f"{n}_var_eps", [P, NT]) for n in ("x", "o", "x1", "y")}
        rstd = {n: sb(f"{n}_rstd", [P, NT]) for n in ("x", "o", "x1", "y")}

        turned = sb("turned", [SQUARE, NB, SQUARE])
        logits = sb("logits", [SQUARE, NB, E])
        logit_max = sb("logit_max", [SQUARE, NB])
        exps = sb("exps", [SQUARE, NB, E])
        exp_sum = sb("exp_sum", [SQUARE, NB])
        exp_rec = sb("exp_rec", [SQUARE, NB])
        route_p = sb("route_p", [SQUARE, NB, E])
        best = sb("best", [SQUARE, NB])
        ties = sb("ties", [SQUARE, NB, E])
        best_tie = sb("best_tie", [SQUARE, NB])
        first_pick = sb("first_pick", [SQUARE, NB, E])
        rest = sb("rest", [SQUARE, NB, E])
        picked = sb("picked", [SQUARE, NB, E])
        coef = turned
        coefT = sb("coefT", [SQUARE, N])
        spread = sb("spread", [P, SPREADS, N])

        middle = sb("middle", [P, 3, 2, N])
        silu_g, gated, act = middle[:, 0], middle[:, 1], middle[:, 2]
        actT = [sb("act_hi", [P, NU, N], F32R), sb("act_lo", [P, NU, N], F32R)]
        out_bias = sb("out_bias", [P, NT])
        stage = [ending[:, 0:KB * E * P], middle[:, :, :, :].rearrange("p k s n -> p (k s n)")[:, 0:KB * E * P]]

        F = [ctx.enter_context(nc.psum_tensor(f"ffn_bank{n}", [P, N], F32)) for n in range(4)]
        A = [ctx.enter_context(nc.psum_tensor(f"attn_bank{n}", [P, N], F32)) for n in range(4)]
        O_BANK = (1, 0)

        def banks_of(what, b):
            for n, early in enumerate(({"v": (F[0], F[1]), "h": (F[0], F[1]), "router": (F[2],)},
                                       {"xn": (F[2], F[3]), "q": (F[0], F[1]), "v": (F[2], F[3])})):
                if b.is_number(n) and what in early:
                    return early[what]
            return {"xn": (A[0], A[1]), "q": (A[2], A[0]), "v": (A[1], A[2]),
                    "h": (A[1], A[2]), "router": (A[3],)}[what]

        ident_set = sem("ident_set")
        constants_done = sem("constants_done")
        qk_loaded, v_loaded, shared_loaded = sem("qk_loaded"), sem("v_loaded"), sem("shared_loaded")
        x_ahead_loaded = sem("x_ahead_loaded")
        gate_loaded, up_loaded, down_loaded = sem("gate_loaded"), sem("up_loaded"), sem("down_loaded")
        qkT_psum, qkT_done, m_psum, m_scaled = (sem("qkT_psum"), sem("qkT_done"), sem("m_psum"), sem("m_scaled"))
        hi_ready = sem("hi_ready")
        ffn_hi_ready = sem("ffn_hi_ready")
        lo_ready = sem("lo_ready")
        ffn_lo_ready = sem("ffn_lo_ready")

        x_loaded = sem("x_loaded")
        x1_copied = sem("x1_copied")
        out_stored = sem("out_stored")

        ln_stats = {n: sem(f"{n}_stats_done") for n in ("x", "o", "x1")}
        ln_moments = {n: sem(f"{n}_moments_done") for n in ("x", "o", "x1")}
        ln_var = {n: sem(f"{n}_var_done") for n in ("x", "o", "x1")}
        ln_rstd = {n: sem(f"{n}_rstd_done") for n in ("x", "o", "x1")}
        xn_ready = sem("xn_ready")
        xnT_psum, xnT_hi, xnT_lo = sem("xnT_psum"), sem("xnT_hi_done"), sem("xnT_lo_done")
        qT_psum, qT_hi, qT_lo = sem("qT_psum"), sem("qT_hi_done"), sem("qT_lo_done")
        v_psum, v_hi, v_lo = sem("v_psum"), sem("v_hi_done"), sem("v_lo_done")
        scores_psum, scores_masked = sem("scores_psum"), sem("scores_masked")
        lo_masked = sem("lo_masked")
        max_done, exp_done = sem("max_done"), sem("exp_done")
        probsT_psum, probsT_hi, probsT_lo = sem("probsT_psum"), sem("probsT_hi_done"), sem("probsT_lo_done")
        o_psum = sem("o_psum")
        sum_sq_done = sem("sum_sq_done")
        x1_done = sem("x1_done")
        h_ready = sem("h_ready")
        hT_psum, hT_hi, hT_lo = sem("hT_psum"), sem("hT_hi_done"), sem("hT_lo_done")
        logitsT_psum, logits_turned, logits_summed = sem("logitsT_psum"), sem("logits_turned"), sem("logits_summed")
        logit_max_done, shifted_done, exps_done = sem("logit_max_done"), sem("shifted_done"), sem("exps_done")
        exp_sum_done, exp_rec_done, route_p_done = sem("exp_sum_done"), sem("exp_rec_done"), sem("route_p_done")
        best_done, equals_done, ties_done, best_tie_done, pick_done = (
            sem("best_done"), sem("equals_done"), sem("ties_done"), sem("best_tie_done"), sem("pick_done"))
        rest_done, picked_done, coef_done = sem("rest_done"), sem("picked_done"), sem("coef_done")
        coef_stored = sem("coef_stored")
        coef_spread = [sem(f"coef_spread{n}") for n in range(SPREADS)]
        coefT_done = sem("coefT_done")

        gate_psum, up_psum = sem("gate_psum"), sem("up_psum")
        silu_done, gated_done, act_done = sem("silu_done"), sem("gated_done"), sem("act_done")
        act_hi_done, act_lo_done = sem("act_hi_done"), sem("act_lo_done")
        y_psum, y_stats_done, y_moments_done, y_var_done, y_rstd_done, y_bias_done, y_norm_done, y_added = (
            sem("y_psum"), sem("y_stats_done"), sem("y_moments_done"), sem("y_var_done"),
            sem("y_rstd_done"), sem("y_bias_done"), sem("y_norm_done"), sem("y_added"))

        HI, LO = 0, 1
        PASSES = ((HI, HI), (HI, LO), (LO, HI))

        def f32(ap):
            return ap.bitcast(F32)

        shared_n = KB * DS
        qkv_st = stage[0][:, 0:KB * 3 * D].rearrange("p (b n) -> p b n", b=KB)
        sh_gate = stage[1][:, 0:shared_n].rearrange("p (b u d) -> p b u d", b=KB, u=SU)
        sh_up = stage[1][:, shared_n:2 * shared_n].rearrange("p (b u d) -> p b u d", b=KB, u=SU)
        sh_down = stage[1][:, 2 * shared_n:2 * shared_n + SU * D].rearrange("p (u n) -> p u n", u=SU)
        r_st = stage[1][:, 2 * shared_n + SU * D:2 * shared_n + SU * D + KB * E].rearrange("p (b e) -> p b e", b=KB)
        ex_gate = stage[0].rearrange("p (b e d) -> p b e d", b=KB, e=E)
        ex_up = stage[1].rearrange("p (b e d) -> p b e d", b=KB, e=E)
        ex_down = stage[0].rearrange("p (e n) -> p e n", e=E)

        x_ahead = spread[:, 0:NT * D // N, :].rearrange("p s (k d) -> p (s k) d", d=D)

        coef_dram = nc.dram_tensor("coef_rows", (E, N), F32).ap()

        block = ctx.enter_context(nc.Block())

        @block.sync
        def _(sp):
            def load_x(b):
                if not b.is_first():
                    sp.wait_ge(x1_done, b.count(2, 0))
                sp.dma_start(x[:, :, :], x_dram[b.index()].rearrange("(t p) d -> p t d", p=P)).then_inc(x_loaded, 16)

            def spread_coef(b):
                sp.wait_ge(coefT_done, b.count(1, 1))
                sp.dma_start(coef_dram, coefT[0:E, :]).then_inc(coef_stored, 16)
                sp.wait_ge(coef_stored, b.count(16, 16))
                for e in range(E):
                    n, turn = e % SPREADS, e // SPREADS
                    if turn:
                        sp.wait_ge(act_done, b.count(NU, SU + e - SPREADS + 1))
                    sp.dma_start(spread[:, n, :], coef_dram[e:e + 1, :].to_broadcast([P, N])) \
                        .then_inc(coef_spread[n], 16)

            def copy_x1(b):
                sp.wait_ge(x1_done, b.count(2, 2))
                if not b.is_first():
                    sp.wait_ge(y_added, b.count(NT, 0))
                sp.dma_start(x1_ffn[:, :, :], x1[:, :, :]).then_inc(x1_copied, 16)

            def store(b):
                sp.wait_ge(y_added, b.count(NT, NT))
                sp.dma_start(out_dram[b.index()].rearrange("(t p) d -> p t d", p=P), y_norm[:, :, :]) \
                    .then_inc(out_stored, 16)

            def store_last(b):
                out = out_dram[b.index()].rearrange("(t p) d -> p t d", p=P)
                sp.wait_ge(y_added, b.count(NT, NT - 1))
                sp.dma_start(out[:, 0:NT - 1, :], y_norm[:, 0:NT - 1, :]).then_inc(out_stored, 16)
                sp.wait_ge(y_added, b.count(NT, NT))
                sp.dma_start(out[:, NT - 1, :], y_norm[:, NT - 1, :]).then_inc(out_stored, 16)

            load_x(Batch(0))
            w_qkv = W_qkv.rearrange("(b p) n -> p b n", p=P)
            sp.dma_start(qkv_st[:, :, 0:2 * D], w_qkv[:, :, 0:2 * D]).then_inc(qk_loaded, 16)
            sp.dma_start(qkv_st[:, :, 2 * D:3 * D], w_qkv[:, :, 2 * D:3 * D]).then_inc(v_loaded, 16)
            sp.dma_start(x_ahead, x_dram[1].rearrange("(t p) d -> p t d", p=P)).then_inc(x_ahead_loaded, 16)
            sp.dma_start(sh_gate, shared_gate.rearrange("(b p) (u d) -> p b u d", p=P, u=SU)).then_inc(shared_loaded, 16)
            sp.dma_start(sh_up, shared_up.rearrange("(b p) (u d) -> p b u d", p=P, u=SU)).then_inc(shared_loaded, 16)
            sp.dma_start(sh_down, shared_down.rearrange("(u p) n -> p u n", p=P)).then_inc(shared_loaded, 16)
            sp.dma_start(r_st, router.rearrange("(b p) e -> p b e", p=P)).then_inc(shared_loaded, 16)
            sp.wait_ge(lo_ready, 1)
            sp.wait_ge(qkT_psum, 2)
            for b in range(KB):
                sp.dma_start(ex_gate[:, b], experts_gate[:, b * P:(b + 1) * P, :].rearrange("e p d -> p e d")) \
                    .then_inc(gate_loaded, 16)
            sp.wait_ge(ffn_lo_ready, 4)
            for b in range(KB):
                sp.dma_start(ex_up[:, b], experts_up[:, b * P:(b + 1) * P, :].rearrange("e p d -> p e d")) \
                    .then_inc(up_loaded, 16)
            sp.wait_ge(ffn_lo_ready, 5)
            sp.dma_start(ex_down, experts_down.rearrange("e p n -> p e n")).then_inc(down_loaded, 16)

            load_x(Batch(0, 1))
            sp.wait_ge(ffn_lo_ready, 7)
            copy_x1(Batch(0))

            def iteration(i, attn):
                spread_coef(Batch(i))
                if attn == 2:
                    load_x(Batch(i, 2))
                if attn:
                    store(Batch(i))
                    copy_x1(Batch(i, 1))
                else:
                    store_last(Batch(i))

            iteration(0, 2)
            with sp.Fori(1, B - 2) as i:
                iteration(i, 2)
            iteration(B - 2, 1)
            iteration(B - 1, 0)
            sp.wait_ge(out_stored, 16 * (B + 1))

        @block.tensor
        def _(pe):
            def split_matmul(out, pairs):
                for n, (lhs, rhs) in enumerate(pairs):
                    for p, (a, b) in enumerate(PASSES):
                        mm = nc.tensor.matmul(out, lhs[a], rhs[b], start=n == 0 and p == 0,
                                              stop=n == len(pairs) - 1 and p == len(PASSES) - 1)
                return mm

            def both(t, *key):
                return [t[HI][key], t[LO][key]]

            def transpose_xn(b):
                pe.wait_ge(xn_ready, b.count(1, 1))
                for k in range(KB):
                    for t in range(NT):
                        mm = nc.tensor.transpose(banks_of("xn", b)[k][:, t * P:(t + 1) * P], xn[:, t, k * P:(k + 1) * P], ident[:, :])
                    mm.then_inc(xnT_psum, 1)

            def project_q(b):
                pe.wait_ge(xnT_lo, b.count(KB, KB))
                if b.is_first():
                    pe.wait_ge(lo_ready, 2)
                elif b.is_number(1):
                    pe.wait_ge(v_lo, b.count(2, 0))
                for m in range(KB):
                    mm = split_matmul(banks_of("q", b)[m][:, :],
                                      [(both(score_w, slice(None), k, slice(m * P, (m + 1) * P)),
                                        both(xnT, slice(None), k, slice(None))) for k in range(KB)])
                    mm.then_inc(qT_psum, 1)

            def project_v(b):
                if b.is_first():
                    pe.wait_ge(xnT_lo, KB)
                    pe.wait_ge(lo_ready, 1)
                early = b.is_first() or b.is_number(1)
                for pair in range(2):
                    if pair == 1 and not early:
                        pe.wait_ge(qT_lo, b.count(KB, 1))
                    for t in (2 * pair, 2 * pair + 1):
                        mm = split_matmul(banks_of("v", b)[pair][:, t % 2 * D:(t % 2 + 1) * D],
                                          [(both(xnT, slice(None), k, slice(t * P, (t + 1) * P)),
                                            both(value_w, slice(None), k, slice(None))) for k in range(KB)])
                    mm.then_inc(v_psum, 1)

            def scores(b, n):
                q = order[n]
                if n == 0:
                    pe.wait_ge(qT_lo, b.count(KB, 2))
                    if b.is_number(1):
                        pe.wait_ge(x1_done, b.count(2, 0))
                elif b.is_first() or b.is_number(1):
                    pass
                elif n < 3:
                    pe.wait_ge(v_lo, b.count(2, n))
                else:
                    pe.wait_ge(logits_turned, b.count(1, 0))
                out = A[n]
                if q == 0:
                    def wide(m):
                        return nc.tensor.matmul(out[:, 0:2 * P].rearrange("p (r n) -> p r n", r=2), qT[HI][:, m, 0:P],
                                                xnT_both[:, :, m, 0:P], start=m == 0, stop=m == KB - 1)

                    wide(0)
                    for m in range(KB):
                        nc.tensor.matmul(out[:, 0:P], qT[LO][:, m, 0:P], xnT[HI][:, m, 0:P],
                                         start=False, stop=False, skip_group_check=True)
                    mm = wide(KB - 1)
                    mm.then_inc(scores_psum, 1)
                    return
                for m in range(KB):
                    for p, (s, r) in enumerate(PASSES):
                        mm = nc.tensor.matmul(out[:, 0:width[q]], qT[s][:, m, q * P:(q + 1) * P],
                                              xnT[r][:, m, 0:width[q]], start=m == 0 and p == 0,
                                              stop=m == KB - 1 and p == len(PASSES) - 1)
                mm.then_inc(scores_psum, 1)

            def transpose_probs(b, n):
                q = order[n]
                pe.wait_ge(exp_done, b.count(NT, n + 1))
                for j in range(q + 1):
                    at = start[q] + j * P
                    mm = nc.tensor.transpose(A[n][:, j * P:(j + 1) * P], probs[:, at:at + P], ident[:, :])
                mm.then_inc(probsT_psum, 1)

            def weigh_values(b, pair):
                pe.wait_ge(probsT_lo, b.count(NT, 2 * pair + 2))
                if pair == 0 and (b.is_first() or b.is_number(1)):
                    pe.wait_ge(v_lo, b.count(2, 2))
                for n in (2 * pair, 2 * pair + 1):
                    q = order[n]
                    mm = split_matmul(A[O_BANK[pair]][:, n % 2 * D:(n % 2 + 1) * D],
                                      [(both(probsT, slice(None), slice(start[q] + j * P, start[q] + (j + 1) * P)),
                                        both(v, slice(None), j, slice(None))) for j in range(q + 1)])
                mm.then_inc(o_psum, 1)

            def transpose_h(b):
                pe.wait_ge(h_ready, b.count(1, 1))
                for k in range(KB):
                    for t in range(NT):
                        mm = nc.tensor.transpose(banks_of("h", b)[k][:, t * P:(t + 1) * P], h[:, t, k * P:(k + 1) * P], ident[:, :])
                    mm.then_inc(hT_psum, 1)

            def route(b):
                if b.is_first():
                    pe.wait_ge(v_lo, 2 + 1)
                pe.wait_ge(hT_lo, b.count(KB, KB))
                if b.is_first():
                    pe.wait_ge(ffn_lo_ready, 4)
                for k in range(KB):
                    for half in (LO, HI):
                        mm = nc.tensor.matmul(banks_of("router", b)[0][:, :], router_w[:, k, :], hT[half][:, k, :],
                                              start=k == 0 and half == LO, stop=k == KB - 1 and half == HI)
                mm.then_inc(logitsT_psum, 1)

            def gate(b, u):
                g = F[2 * (u % 2)]
                if u >= 2:
                    pe.wait_ge(silu_done, b.count(NU, u - 1))
                elif not b.is_first():
                    pe.wait_ge(y_norm_done, b.count(NT, 2 * u + 1 - NT))
                split_matmul(g[:, :], [(both(gate_w, slice(None), k, u, slice(None)),
                                        both(hT, slice(None), k, slice(None))) for k in range(KB)]) \
                    .then_inc(gate_psum, 1)

            def up(b, u):
                to = F[2 * (u % 2) + 1]
                if u >= 2 + SU:
                    pe.wait_ge(gated_done, b.count(E, u - 1 - SU))
                elif u >= 2:
                    pe.wait_ge(act_done, b.count(NU, u - 1))
                elif not b.is_first():
                    pe.wait_ge(y_norm_done, b.count(NT, 2 * u + 2 - NT))
                split_matmul(to[:, :], [(both(up_w, slice(None), k, u, slice(None)),
                                         both(hT, slice(None), k, slice(None))) for k in range(KB)]) \
                    .then_inc(up_psum, 1)

            def first_units(b):
                route(b)
                gate(b, 0)
                up(b, 0)
                pe.wait_ge(v_lo, 2 * 2)
                pe.wait_ge(logits_turned, 1)
                gate(b, 1)
                up(b, 1)
                pe.wait_ge(ffn_lo_ready, 6)

            def down(b, t, units):
                for u in units:
                    for p, (s, r) in enumerate(PASSES):
                        mm = nc.tensor.matmul(F[t][:, 0:D], actT[s][:, u, t * P:(t + 1) * P], down_w[r][:, u, :],
                                              start=u == 0 and p == 0, stop=u == NU - 1 and p == len(PASSES) - 1)
                return mm

            def down_first_two(b):
                early = range(NU - 1)
                pe.wait_ge(act_lo_done, b.count(NU, NU - 2))
                pe.wait_ge(silu_done, b.count(NU, NU - 1))
                down(b, 0, early[:-1])
                pe.wait_ge(gated_done, b.count(E, E - 1))
                down(b, 1, early[:-1])
                pe.wait_ge(act_lo_done, b.count(NU, NU - 1))
                down(b, 0, early[-1:])
                down(b, 1, early[-1:])
                pe.wait_ge(act_lo_done, b.count(NU, NU))
                for t in range(2):
                    down(b, t, [NU - 1]).then_inc(y_psum, 1)

            pe.wait_ge(ident_set, 2)
            pe.wait_ge(qk_loaded, 16)
            for side in range(2):
                for d in range(KB):
                    for k in range(KB):
                        mm = nc.tensor.transpose(F[side][:, d * D + k * P:d * D + (k + 1) * P],
                                                 qkv_st[:, k, side * D + d * P:side * D + (d + 1) * P], ident[:, :])
                mm.then_inc(qkT_psum, 1)
            pe.wait_ge(qkT_done, 2)
            hf = h[:, :, :].rearrange("p t d -> p (t d)")
            for i in range(KB):
                if i == 1:
                    transpose_xn(Batch(0))
                for d in range(KB):
                    mm = nc.tensor.matmul(F[2][:, i * D:(i + 1) * D], hf[:, d * D + i * P:d * D + (i + 1) * P],
                                          hf[:, N + d * D:N + (d + 1) * D], start=d == 0, stop=d == KB - 1)
            mm.then_inc(m_psum, 1)

            def attention_alone(b):
                ahead = Batch(0, 1)
                project_v(b)
                project_q(b)
                for n in range(NT):
                    scores(b, n)
                for n in range(NT):
                    transpose_probs(b, n)
                transpose_xn(ahead)
                weigh_values(b, 0)
                weigh_values(b, 1)
                project_q(ahead)
                project_v(ahead)
                for n in range(NT):
                    scores(ahead, n)
                transpose_h(b)

            def iteration(i, attn):
                b, c = Batch(i), Batch(i, 1)
                if b.is_first():
                    first_units(b)
                for u in range(2 if b.is_first() else 0, NU):
                    gate(b, u)
                    up(b, u)
                    if attn and u == 1:
                        project_q(c)
                    if attn and u == 2 and not b.is_first():
                        project_v(c)
                    if attn and u == 3 and not b.is_first():
                        scores(c, 0)
                        scores(c, 1)
                    if attn and u == 4 and not b.is_first():
                        scores(c, 2)
                        scores(c, 3)
                    if attn and u == 5:
                        transpose_probs(c, 0)
                        transpose_probs(c, 1)
                    if attn and u == 6:
                        transpose_probs(c, 2)
                        transpose_probs(c, 3)
                    if attn and u == 7:
                        weigh_values(c, 0)
                    if attn and u == 8:
                        weigh_values(c, 1)
                if b.is_first():
                    pe.wait_ge(ffn_lo_ready, 7)
                down_first_two(b)
                down(b, 2, range(NU // 2))
                if attn:
                    transpose_h(c)
                down(b, 2, range(NU // 2, NU)).then_inc(y_psum, 1)
                down(b, 3, range(3))
                if attn:
                    route(c)
                down(b, 3, range(3, NU)).then_inc(y_psum, 1)
                if attn == 2:
                    transpose_xn(Batch(i, 2))

            attention_alone(Batch(0))
            iteration(0, 2)
            with pe.Fori(1, B - 2) as i:
                iteration(i, 2)
            iteration(B - 2, 1)
            iteration(B - 1, 0)

        @block.scalar
        def _(act_e):
            def xnT_his(b):
                for k in range(KB):
                    act_e.wait_ge(xnT_psum, b.count(KB, k + 1))
                    nc.scalar.activation(xnT[HI][:, k, :], banks_of("xn", b)[k][:, :], ACT.Copy) \
                        .then_inc(xnT_hi, 1)

            def qT_his(b):
                for m in range(KB):
                    act_e.wait_ge(qT_psum, b.count(KB, m + 1))
                    nc.scalar.activation(qT[HI][:, m, :], banks_of("q", b)[m][:, :], ACT.Copy) \
                        .then_inc(qT_hi, 1)

            def v_his(b):
                for pair in range(2):
                    act_e.wait_ge(v_psum, b.count(2, pair + 1))
                    nc.scalar.activation(v[HI][:, 2 * pair:2 * pair + 2, :].rearrange("p t d -> p (t d)"), banks_of("v", b)[pair][:, :],
                                         ACT.Copy) \
                        .then_inc(v_hi, 1)

            def exp(b, n):
                q = order[n]
                act_e.wait_ge(max_done, b.count(NT, n + 1))
                nc.scalar.activation(probs[:, start[q]:start[q] + width[q]], A[n][:, 0:width[q]], ACT.Exp,
                                     bias=neg_max[:, q:q + 1], accum_out=row_sum[:, q:q + 1]).then_inc(exp_done, 1)

            def probsT_his(b, n):
                q = order[n]
                act_e.wait_ge(probsT_psum, b.count(NT, n + 1))
                nc.scalar.activation(probsT[HI][:, start[q]:start[q] + width[q]], A[n][:, 0:width[q]], ACT.Copy) \
                    .then_inc(probsT_hi, 1)

            def hT_his(b):
                for k in range(KB):
                    act_e.wait_ge(hT_psum, b.count(KB, k + 1))
                    nc.scalar.activation(hT[HI][:, k, :], banks_of("h", b)[k][:, :], ACT.Copy) \
                        .then_inc(hT_hi, 1)

            def router_exp(b):
                act_e.wait_ge(shifted_done, b.count(1, 1))
                nc.scalar.activation(exps[:, :, :], logits[:, :, :], ACT.Exp).then_inc(exps_done, 1)

            def silu(b, u):
                act_e.wait_ge(gate_psum, b.count(NU, u + 1))
                if u >= 2 + SU:
                    act_e.wait_ge(gated_done, b.count(E, u - 1 - SU))
                elif u >= 2:
                    act_e.wait_ge(act_done, b.count(NU, u - 1))
                nc.scalar.activation(silu_g[:, u % 2, :], F[2 * (u % 2)][:, :], ACT.Silu).then_inc(silu_done, 1)

            def act_hi(b, u):
                act_e.wait_ge(act_done, b.count(NU, u + 1))
                nc.scalar.activation(actT[HI][:, u, :], act[:, u % 2, :], ACT.Copy) \
                    .then_inc(act_hi_done, 1)

            def normalise_y(b, t):
                act_e.wait_ge(y_bias_done, b.count(NT, t + 1))
                if not b.is_first():
                    act_e.wait_ge(out_stored, b.count(16, 0))
                nc.scalar.activation(y_norm[:, t, :], F[t][:, 0:D], ACT.Identity, bias=out_bias[:, t:t + 1],
                                     scale=rstd["y"][:, t:t + 1]).then_inc(y_norm_done, 1)

            def weights_hi(loaded, value, *pairs):
                act_e.wait_ge(loaded, value)
                for dst, src in pairs:
                    nc.scalar.activation(dst, src, ACT.Copy).then_inc(ffn_hi_ready, 1)

            def attention_alone(b):
                ahead = Batch(0, 1)
                xnT_his(b)
                act_e.wait_ge(constants_done, 1)
                weights_hi(shared_loaded, 64, (gate_w[HI][:, :, 0:SU, :], sh_gate), (up_w[HI][:, :, 0:SU, :], sh_up),
                           (down_w[HI][:, 0:SU, :], sh_down), (router_w[:, :, 0:E], r_st))
                v_his(b)
                qT_his(b)
                weights_hi(gate_loaded, 16 * KB, (gate_w[HI][:, :, SU:, :], ex_gate))
                for n in range(NT):
                    exp(b, n)
                for n in range(NT):
                    probsT_his(b, n)
                xnT_his(ahead)
                weights_hi(up_loaded, 16 * KB, (up_w[HI][:, :, SU:, :], ex_up))
                qT_his(ahead)
                v_his(ahead)
                weights_hi(down_loaded, 16, (down_w[HI][:, SU:, :], ex_down))
                hT_his(b)
                exp(ahead, 0)
                exp(ahead, 1)
                router_exp(b)
                exp(ahead, 2)
                exp(ahead, 3)
                act_e.wait_ge(ffn_lo_ready, 6)
                silu(b, 0)
                silu(b, 1)
                act_hi(b, 0)

            def iteration(i, attn):
                b, c = Batch(i), Batch(i, 1)
                for u in range(2 if b.is_first() else 0, NU):
                    silu(b, u)
                    if u >= 1:
                        act_hi(b, u - 1)
                    if attn and u == 1:
                        qT_his(c)
                    if attn and u == 2 and not b.is_first():
                        v_his(c)
                    if attn and u == 4 and not b.is_first():
                        for n in range(NT):
                            exp(c, n)
                    if attn and u == 5:
                        probsT_his(c, 0)
                        probsT_his(c, 1)
                    if attn and u == 6:
                        probsT_his(c, 2)
                        probsT_his(c, 3)
                act_hi(b, NU - 1)
                if attn:
                    hT_his(c)
                normalise_y(b, 0)
                normalise_y(b, 1)
                if attn:
                    router_exp(c)
                normalise_y(b, 2)
                if attn == 2:
                    xnT_his(Batch(i, 2))
                normalise_y(b, 3)

            hf = h[:, :, :].rearrange("p t d -> p (t d)")
            for side in range(2):
                act_e.wait_ge(qkT_psum, side + 1)
                nc.scalar.activation(hf[:, side * N:(side + 1) * N], F[side][:, :], ACT.Copy).then_inc(qkT_done, 1)
            attention_alone(Batch(0))
            iteration(0, 2)
            with act_e.Fori(1, B - 2) as i:
                iteration(i, 2)
            iteration(B - 2, 1)
            iteration(B - 1, 0)

        @block.vector
        def _(dve):
            def moments_of(name, b, sources):
                for t in range(NT):
                    ins = nc.vector.bn_stats(stats[name][:, t, :], sources[t])
                ins.then_inc(ln_stats[name], 1)
                finish_moments(name, b)

            def finish_moments(name, b):
                dve.wait_ge(ln_stats[name], b.count(1, 1))
                nc.vector.memset(scratch[:, 0:1], 0.0)
                for t in range(NT):
                    ins = nc.vector.bn_aggr(moments[name][:, t, :], stats[name][:, t, :])
                ins.then_inc(ln_moments[name], 1)
                dve.wait_ge(ln_moments[name], b.count(1, 1))
                if name == "o":
                    dve.wait_ge(sum_sq_done, b.count(1, 1))
                    nc.vector.tensor_tensor(var_eps[name][:, :], moments[name][:, :, 1], sum_sq_eps[:, :], ALU.add) \
                        .then_inc(ln_var[name], 1)
                else:
                    nc.vector.tensor_scalar(var_eps[name][:, :], moments[name][:, :, 1], EPS, None, ALU.add) \
                        .then_inc(ln_var[name], 1)

            def normalise(name, b, dst, src, sem_out):
                dve.wait_ge(ln_rstd[name], b.count(1, 1))
                for t in range(NT):
                    ins = nc.vector.tensor_scalar(dst[:, t, :], src(t), moments[name][:, t, 0:1],
                                                  rstd[name][:, t:t + 1], ALU.subtract, ALU.mult)
                ins.then_inc(sem_out, 1)

            def norm_x_stats(b, x=x):
                if b.is_number(1):
                    dve.wait_ge(x_ahead_loaded, 16)
                else:
                    dve.wait_ge(x_loaded, b.count(16, 16))
                moments_of("x", b, [x[:, t, :] for t in range(NT)])

            def norm_x(b, x=x):
                if not b.is_first():
                    dve.wait_ge(xnT_psum, b.count(KB, 0))
                normalise("x", b, xn, lambda t: x[:, t, :], xn_ready)

            def xnT_los(b):
                for k in range(KB):
                    dve.wait_ge(xnT_hi, b.count(KB, k + 1))
                    nc.vector.tensor_tensor(xnT[LO][:, k, :], banks_of("xn", b)[k][:, :], f32(xnT[HI][:, k, :]),
                                            ALU.subtract).then_inc(xnT_lo, 1)

            def qT_los(b, which=range(KB)):
                for m in which:
                    dve.wait_ge(qT_hi, b.count(KB, m + 1))
                    nc.vector.tensor_tensor(qT[LO][:, m, :], banks_of("q", b)[m][:, :], f32(qT[HI][:, m, :]),
                                            ALU.subtract).then_inc(qT_lo, 1)

            def v_los(b, which=range(2)):
                for pair in which:
                    at = lambda t: t[:, 2 * pair:2 * pair + 2, :].rearrange("p t d -> p (t d)")
                    dve.wait_ge(v_hi, b.count(2, pair + 1))
                    nc.vector.tensor_tensor(at(v[LO]), banks_of("v", b)[pair][:, :], f32(at(v[HI])),
                                            ALU.subtract).then_inc(v_lo, 1)

            def row_max(b, *tiles):
                for n in tiles:
                    q = order[n]
                    dve.wait_ge(scores_psum, b.count(NT, n + 1))
                    diagonal = A[n][:, q * P:(q + 1) * P]
                    if q == 0:
                        nc.vector.tensor_tensor(scores_lo[:, :], A[n][:, P:2 * P], causal[:, :], ALU.add) \
                            .then_inc(lo_masked, 1)
                        dve.wait_ge(lo_masked, b.count(1, 1))
                        nc.vector.tensor_tensor(diagonal, diagonal, scores_lo[:, :], ALU.add).then_inc(scores_masked, 1)
                        continue
                    nc.vector.tensor_tensor(diagonal, diagonal, causal[:, :], ALU.add).then_inc(scores_masked, 1)
                for n in tiles:
                    q = order[n]
                    dve.wait_ge(scores_masked, b.count(NT, n + 1))
                    nc.vector.tensor_reduce(neg_max[:, q:q + 1], A[n][:, 0:width[q]], AX.X, ALU.max, negate=True) \
                        .then_inc(max_done, 1)

            def probsT_los(b, n):
                q = order[n]
                at = slice(start[q], start[q] + width[q])
                dve.wait_ge(probsT_hi, b.count(NT, n + 1))
                nc.vector.tensor_tensor(probsT[LO][:, at], A[n][:, 0:width[q]], f32(probsT[HI][:, at]),
                                        ALU.subtract).then_inc(probsT_lo, 1)

            def o_of(q):
                n = order.index(q)
                return A[O_BANK[n // 2]][:, n % 2 * D:(n % 2 + 1) * D]

            def o_stats(b, pair):
                dve.wait_ge(o_psum, b.count(2, pair + 1))
                for n in (2 * pair, 2 * pair + 1):
                    ins = nc.vector.bn_stats(stats["o"][:, order[n], :], o_of(order[n]))
                if pair == 0:
                    nc.vector.scalar_tensor_tensor(out=sum_sq_eps[:, :], in0=row_sum[:, :], scalar=EPS,
                                                   in1=row_sum[:, :], op0=ALU.mult, op1=ALU.mult) \
                        .then_inc(sum_sq_done, 1)
                else:
                    ins.then_inc(ln_stats["o"], 1)

            def make_x1(b):
                dve.wait_ge(ln_rstd["o"], b.count(1, 1))
                if b.is_number(1):
                    dve.wait_ge(x_loaded, b.count(16, 16))
                if not b.is_first():
                    dve.wait_ge(x1_copied, b.count(16, 0))
                nc.vector.scalar_tensor_tensor(out=x1[:, :, D], in0=moments["o"][:, :, 0], scalar=-1.0,
                                               in1=rstd["o"][:, :], op0=ALU.mult, op1=ALU.mult)
                for pair in range(2):
                    for n in (2 * pair, 2 * pair + 1):
                        q = order[n]
                        ins = nc.vector.scalar_tensor_tensor(out=x1[:, q, 0:D], in0=o_of(q), scalar=rstd["o"][:, q:q + 1],
                                                             in1=x[:, q, :], op0=ALU.mult, op1=ALU.add)
                    ins.then_inc(x1_done, 1)

            def x1_stats(b):
                dve.wait_ge(x1_done, b.count(2, 2))
                moments_of("x1", b, [x1[:, t, 0:D] for t in range(NT)])

            def norm_x1(b):
                normalise("x1", b, h, lambda t: x1[:, t, 0:D], h_ready)

            def hT_los(b):
                for k in range(KB):
                    dve.wait_ge(hT_hi, b.count(KB, k + 1))
                    nc.vector.tensor_tensor(hT[LO][:, k, :], banks_of("h", b)[k][:, :], f32(hT[HI][:, k, :]),
                                            ALU.subtract).then_inc(hT_lo, 1)

            def bcast(ap, shape, axis):
                return ap.unsqueeze(axis).to_broadcast(shape)

            def route_logits(b):
                dve.wait_ge(logitsT_psum, b.count(1, 1))
                nc.vector.transpose(turned[:, :, :].rearrange("p b k -> p (b k)"), banks_of("router", b)[0][0:SQUARE, :]) \
                    .then_inc(logits_turned, 1)
                dve.wait_ge(logits_turned, b.count(1, 1))
                nc.vector.tensor_tensor(logits[:, :, :], turned[:, :, 0:E], turned[:, :, E:2 * E], ALU.add) \
                    .then_inc(logits_summed, 1)
                dve.wait_ge(logits_summed, b.count(1, 1))
                nc.vector.tensor_reduce(logit_max[:, :], logits[:, :, :], AX.X, ALU.max).then_inc(logit_max_done, 1)
                dve.wait_ge(logit_max_done, b.count(1, 1))
                nc.vector.tensor_tensor(logits[:, :, :], logits[:, :, :], bcast(logit_max[:, :], [SQUARE, NB, E], 2),
                                        ALU.subtract).then_inc(shifted_done, 1)

            def find_best(values):
                nc.vector.tensor_reduce(best[:, :], values[:, :, :], AX.X, ALU.max).then_inc(best_done, 1)

            def equal_best(b, pick, values):
                dve.wait_ge(best_done, b.count(TOP_K, pick + 1))
                nc.vector.tensor_tensor(ties[:, :, :], values[:, :, :], bcast(best[:, :], [SQUARE, NB, E], 2),
                                        ALU.is_equal).then_inc(equals_done, 1)

            def take_first(b, pick, out):
                dve.wait_ge(equals_done, b.count(TOP_K, pick + 1))
                nc.vector.tensor_tensor(ties[:, :, :], ties[:, :, :], bcast(preference[:, :], [SQUARE, NB, E], 1),
                                        ALU.mult).then_inc(ties_done, 1)
                dve.wait_ge(ties_done, b.count(TOP_K, pick + 1))
                nc.vector.tensor_reduce(best_tie[:, :], ties[:, :, :], AX.X, ALU.max).then_inc(best_tie_done, 1)
                dve.wait_ge(best_tie_done, b.count(TOP_K, pick + 1))
                nc.vector.tensor_tensor(out[:, :, :], ties[:, :, :], bcast(best_tie[:, :], [SQUARE, NB, E], 2),
                                        ALU.is_equal).then_inc(pick_done, 1)

            def route_sum_best(b):
                dve.wait_ge(exps_done, b.count(1, 1))
                nc.vector.tensor_reduce(exp_sum[:, :], exps[:, :, :], AX.X, ALU.add).then_inc(exp_sum_done, 1)
                find_best(exps)

            def route_equal_best(b):
                dve.wait_ge(exp_sum_done, b.count(1, 1))
                nc.vector.reciprocal(exp_rec[:, :], exp_sum[:, :]).then_inc(exp_rec_done, 1)
                equal_best(b, 0, exps)

            def route_first_pick(b):
                take_first(b, 0, first_pick)
                dve.wait_ge(exp_rec_done, b.count(1, 1))
                nc.vector.tensor_tensor(route_p[:, :, :], exps[:, :, :], bcast(exp_rec[:, :], [SQUARE, NB, E], 2),
                                        ALU.mult).then_inc(route_p_done, 1)

            def route_second_pick(b):
                dve.wait_ge(pick_done, b.count(TOP_K, 1))
                nc.vector.scalar_tensor_tensor(out=rest[:, :, :], in0=first_pick[:, :, :], scalar=-2.0,
                                               in1=exps[:, :, :], op0=ALU.mult, op1=ALU.add).then_inc(rest_done, 1)
                dve.wait_ge(rest_done, b.count(1, 1))
                find_best(rest)
                equal_best(b, 1, rest)
                take_first(b, 1, picked)
                dve.wait_ge(pick_done, b.count(TOP_K, 2))
                nc.vector.tensor_tensor(picked[:, :, :], first_pick[:, :, :], picked[:, :, :], ALU.add) \
                    .then_inc(picked_done, 1)
                dve.wait_ge(picked_done, b.count(1, 1))
                dve.wait_ge(route_p_done, b.count(1, 1))
                nc.vector.tensor_tensor(coef[:, :, 0:E], picked[:, :, :], route_p[:, :, :], ALU.mult) \
                    .then_inc(coef_done, 1)
                dve.wait_ge(coef_done, b.count(1, 1))
                if not b.is_first():
                    dve.wait_ge(coef_stored, b.count(16, 0))
                nc.vector.transpose(coefT[:, :], coef[:, :, :].rearrange("p b k -> p (b k)")).then_inc(coefT_done, 1)

            def hidden(b, u):
                dve.wait_ge(silu_done, b.count(NU, u + 1))
                dve.wait_ge(up_psum, b.count(NU, u + 1))
                up = F[2 * (u % 2) + 1]
                if u < SU:
                    if b.reaches(u - 1):
                        dve.wait_ge(act_lo_done, b.count(NU, u - 1))
                    nc.vector.tensor_tensor(act[:, u % 2, :], up[:, :], silu_g[:, u % 2, :], ALU.mult) \
                        .then_inc(act_done, 1)
                    return
                nc.vector.tensor_tensor(gated[:, u % 2, :], up[:, :], silu_g[:, u % 2, :], ALU.mult) \
                    .then_inc(gated_done, 1)
                dve.wait_ge(gated_done, b.count(E, u - SU + 1))
                n, turn = (u - SU) % SPREADS, (u - SU) // SPREADS
                dve.wait_ge(coef_spread[n], b.count(16 * spread_turns[n], 16 * (turn + 1)))
                if b.reaches(u - 1):
                    dve.wait_ge(act_lo_done, b.count(NU, u - 1))
                nc.vector.tensor_tensor(act[:, u % 2, :], spread[:, n, :], gated[:, u % 2, :], ALU.mult).then_inc(act_done, 1)

            def y_moments(b, t):
                dve.wait_ge(y_psum, b.count(NT, t + 1))
                nc.vector.bn_stats(stats["y"][:, t, :], F[t][:, 0:D]).then_inc(y_stats_done, 1)
                dve.wait_ge(y_stats_done, b.count(NT, t + 1))
                nc.vector.memset(scratch[:, 1:2], 0.0)
                nc.vector.bn_aggr(moments["y"][:, t, :], stats["y"][:, t, :]).then_inc(y_moments_done, 1)
                dve.wait_ge(y_moments_done, b.count(NT, t + 1))
                nc.vector.tensor_scalar(var_eps["y"][:, t:t + 1], moments["y"][:, t, 1:2], EPS, None, ALU.add) \
                    .then_inc(y_var_done, 1)

            def y_bias(b, t):
                dve.wait_ge(y_rstd_done, b.count(NT, t + 1))
                if t == 0:
                    dve.wait_ge(x1_copied, b.count(16, 16))
                nc.vector.scalar_tensor_tensor(out=out_bias[:, t:t + 1], in0=moments["y"][:, t, 0:1],
                                               scalar=rstd["y"][:, t:t + 1], in1=x1_ffn[:, t, D:D + 1],
                                               op0=ALU.mult, op1=ALU.subtract, reverse1=True).then_inc(y_bias_done, 1)

            def split(n, dst, src):
                nc.vector.tensor_copy(dst[HI], src).then_inc(hi_ready, 1)
                dve.wait_ge(hi_ready, n)
                nc.vector.tensor_tensor(dst[LO], src, f32(dst[HI]), ALU.subtract).then_inc(lo_ready, 1)

            norm_x_stats(Batch(0))
            dve.wait_ge(constants_done, 1)
            dve.wait_ge(v_loaded, 16)
            split(1, [value_w[HI][:, :, :], value_w[LO][:, :, :]], qkv_st[:, :, 2 * D:3 * D])
            norm_x(Batch(0))
            norm_x_stats(Batch(0, 1), x_ahead)
            xnT_los(Batch(0))
            dve.wait_ge(m_psum, 1)
            m_sc = probs[:, 0:KB * D].rearrange("p (b d) -> p b d", b=KB)
            nc.vector.tensor_scalar(m_sc, F[2][:, :].rearrange("p (b d) -> p b d", b=KB), SCALE, None, ALU.mult) \
                .then_inc(m_scaled, 1)
            dve.wait_ge(m_scaled, 1)
            split(2, [score_w[HI][:, :, :], score_w[LO][:, :, :]], m_sc)
            norm_x(Batch(0, 1), x_ahead)

            def attention_alone(b):
                ahead = Batch(0, 1)
                v_los(b)
                qT_los(b)
                for n in range(NT):
                    row_max(b, n)
                for n in range(NT):
                    probsT_los(b, n)
                xnT_los(ahead)
                o_stats(b, 0)
                o_stats(b, 1)
                finish_moments("o", b)
                qT_los(ahead, [0])
                make_x1(b)
                qT_los(ahead, [1])
                x1_stats(b)
                v_los(ahead, [0])
                norm_x1(b)
                v_los(ahead, [1])
                hT_los(b)
                row_max(ahead, 0, 1)
                route_logits(b)
                row_max(ahead, 2, 3)
                route_sum_best(b)
                route_equal_best(b)
                route_first_pick(b)

            def iteration(i, attn):
                b, c, d = Batch(i), Batch(i, 1), Batch(i, 2)
                for u in range(NU):
                    if u == 1:
                        route_second_pick(b)
                    if attn and u == 1 and not b.is_first():
                        qT_los(c)
                    if attn and u == 2 and not b.is_first():
                        v_los(c)
                    hidden(b, u)
                    if attn and u == 3 and not b.is_first():
                        row_max(c, 0, 1)
                    if attn and u == 4 and not b.is_first():
                        row_max(c, 2, 3)
                    if attn and u == 5:
                        probsT_los(c, 0)
                        probsT_los(c, 1)
                    if attn and u == 6:
                        probsT_los(c, 2)
                        probsT_los(c, 3)
                    if attn and u == 7:
                        o_stats(c, 0)
                    if attn and u == 8:
                        o_stats(c, 1)
                        finish_moments("o", c)
                if attn:
                    make_x1(c)
                    x1_stats(c)
                    norm_x1(c)
                if attn == 2:
                    norm_x_stats(d)
                if attn:
                    hT_los(c)
                y_moments(b, 0)
                y_moments(b, 1)
                if attn == 2:
                    norm_x(d)
                y_bias(b, 0)
                y_bias(b, 1)
                if attn:
                    route_logits(c)
                y_moments(b, 2)
                y_moments(b, 3)
                y_bias(b, 2)
                if attn:
                    route_sum_best(c)
                    route_equal_best(c)
                y_bias(b, 3)
                if attn == 2:
                    xnT_los(d)
                if attn:
                    route_first_pick(c)

            attention_alone(Batch(0))
            iteration(0, 2)
            with dve.Fori(1, B - 2) as i:
                iteration(i, 2)
            iteration(B - 2, 1)
            iteration(B - 1, 0)

        @block.gpsimd
        def _(pool):
            def rstd_of(name, b):
                pool.wait_ge(ln_var[name], b.count(1, 1))
                nc.gpsimd.tensor_tensor(rstd[name][:, :], var_eps[name][:, :], neg_half[:, :], ALU.pow) \
                    .then_inc(ln_rstd[name], 1)

            def act_lo(b, u):
                pool.wait_ge(act_hi_done, b.count(NU, u + 1))
                nc.gpsimd.tensor_tensor(actT[LO][:, u, :], act[:, u % 2, :], f32(actT[HI][:, u, :]), ALU.subtract) \
                    .then_inc(act_lo_done, 1)

            def y_rstd(b, t):
                pool.wait_ge(y_var_done, b.count(NT, t + 1))
                nc.gpsimd.tensor_tensor(rstd["y"][:, t:t + 1], var_eps["y"][:, t:t + 1], neg_half[:, 0:1], ALU.pow) \
                    .then_inc(y_rstd_done, 1)

            def y_add(b, t):
                pool.wait_ge(y_norm_done, b.count(NT, t + 1))
                nc.gpsimd.tensor_tensor(y_norm[:, t, :], y_norm[:, t, :], x1_ffn[:, t, 0:D], ALU.add) \
                    .then_inc(y_added, 1)

            nc.gpsimd.memset(ident[:, :], 0.0).then_inc(ident_set, 1)
            pool.wait_ge(ident_set, 1)
            nc.gpsimd.affine_select(out=ident[:, :], in_=ident[:, :], compare_op=ALU.not_equal, fill=1.0, base=0,
                                    pattern=[[-1, P]], channel_multiplier=1).then_inc(ident_set, 1)
            nc.gpsimd.memset(neg_half[:, :], -0.5).then_inc(ident_set, 1)
            nc.gpsimd.memset(causal[:, :], 0.0).then_inc(ident_set, 1)
            for e in range(E):
                nc.gpsimd.memset(preference[:, e:e + 1], float(E - e))
            nc.gpsimd.memset(f32(router_w[:, :, :]), 0.0)
            pool.wait_ge(ident_set, 4)
            nc.gpsimd.affine_select(out=causal[:, :], in_=causal[:, :], compare_op=ALU.is_ge, fill=MASKED, base=0,
                                    pattern=[[-1, P]], channel_multiplier=1).then_inc(constants_done, 1)

            def lo_half(n, dst, src, hi):
                pool.wait_ge(ffn_hi_ready, n)
                nc.gpsimd.tensor_tensor(dst, src, f32(hi), ALU.subtract).then_inc(ffn_lo_ready, 1)

            rstd_of("x", Batch(0))
            rstd_of("x", Batch(0, 1))
            lo_half(1, gate_w[LO][:, :, 0:SU, :], sh_gate, gate_w[HI][:, :, 0:SU, :])
            lo_half(2, up_w[LO][:, :, 0:SU, :], sh_up, up_w[HI][:, :, 0:SU, :])
            lo_half(3, down_w[LO][:, 0:SU, :], sh_down, down_w[HI][:, 0:SU, :])
            lo_half(4, router_w[:, :, E:2 * E], r_st, router_w[:, :, 0:E])
            lo_half(5, gate_w[LO][:, :, SU:, :], ex_gate, gate_w[HI][:, :, SU:, :])
            rstd_of("o", Batch(0))
            rstd_of("x1", Batch(0))
            lo_half(6, up_w[LO][:, :, SU:, :], ex_up, up_w[HI][:, :, SU:, :])
            lo_half(7, down_w[LO][:, SU:, :], ex_down, down_w[HI][:, SU:, :])

            def iteration(i, attn):
                b, c, d = Batch(i), Batch(i, 1), Batch(i, 2)
                for u in range(NU):
                    if u == NU - 2 and attn:
                        rstd_of("o", c)
                    act_lo(b, u)
                if attn:
                    rstd_of("x1", c)
                if attn == 2:
                    rstd_of("x", d)
                y_rstd(b, 0)
                y_rstd(b, 1)
                y_add(b, 0)
                y_add(b, 1)
                y_rstd(b, 2)
                y_rstd(b, 3)
                y_add(b, 2)
                y_add(b, 3)

            iteration(0, 2)
            with pool.Fori(1, B - 2) as i:
                iteration(i, 2)
            iteration(B - 2, 1)
            iteration(B - 1, 0)


_INS = ["L0_attn_x", "L0_attn_W_qkv", "L0_ffn_router", "L0_ffn_experts_gate", "L0_ffn_experts_up",
        "L0_ffn_experts_down", "L0_ffn_shared_gate", "L0_ffn_shared_up", "L0_ffn_shared_down"]


def kernel(**inputs):
    import numpy as np
    import concourse.bacc as bacc
    from concourse.bass_utils import run_bass_kernel_spmd

    nc = bacc.Bacc("TRN2", target_bir_lowering=False, num_devices=1)
    arrays, args = {}, []
    for name in _INS:
        a = np.ascontiguousarray(inputs[name])
        arrays[f"in_{name}"] = a
        args.append(nc.dram_tensor(f"in_{name}", a.shape, mybir.dt.from_np(a.dtype), kind="ExternalInput").ap())
    x_shape = inputs["L0_attn_x"].shape
    args.append(nc.dram_tensor("out_x", x_shape, F32, kind="ExternalOutput").ap())
    layer_kernel(nc, *args)
    r = run_bass_kernel_spmd(nc, [arrays], core_ids=[0])
    return r.results[0]["out_x"]
```
